# Optimizing a Trainium2 kernel written in Bass

```python
import numpy as np
import jax
import jax.numpy as jnp

def _softmax(x, axis=-1):
    return jax.nn.softmax(x, axis=axis)

def _gelu(x):
    return jax.nn.gelu(x, approximate=True)

def _silu(x):
    return jax.nn.silu(x)

def _sigmoid(x):
    return jax.nn.sigmoid(x)

def _layernorm(x, axis=-1, eps=1e-05):
    m = jnp.mean(x, axis=axis, keepdims=True)
    v = jnp.var(x, axis=axis, keepdims=True)
    return (x - m) / jnp.sqrt(v + eps)

def _scatter_add(tgt, idx, src, axis=0):
    return tgt.at[idx].add(src)

def _segment_sum(src, seg, n):
    return jax.ops.segment_sum(src, seg, n)
kernel_name = 'mk_hybrid_d1_jaxref_r8_54b01c'

def setup_inputs(seed: int=0):
    np.random.seed(seed)
    _w = jnp.asarray

    def _L0_attn_a_setup():
        import jax, jax.numpy as jnp
        import numpy as np
        B, T, D, H = (4, 256, 128, 16)
        HD = D // H
        ROPE_BASE = 10000.0

        def rotate_half(x):
            x1 = x[..., ::2]
            x2 = x[..., 1::2]
            return jnp.stack((-x2, x1), axis=-1).reshape(x.shape)

        def rope_tables(seq_len, dim, dtype=jnp.float32):
            inv = 1.0 / ROPE_BASE ** (jnp.arange(0, dim, 2, dtype=jnp.float32) / dim)
            t = jnp.arange(seq_len, dtype=jnp.float32)
            freqs = jnp.einsum('i,j->ij', t, inv)
            emb = jnp.concatenate((freqs, freqs), axis=-1)
            return (jnp.cos(emb).astype(dtype)[None, None], jnp.sin(emb).astype(dtype)[None, None])
        key = jax.random.key(seed)
        ks = jax.random.split(key, 9)
        s = 0.02
        return {'x': jax.random.normal(ks[0], (B, T, D), jnp.float32), 'Wq': jax.random.normal(ks[1], (D, D), jnp.float32) * s, 'bq': jnp.zeros((D,), jnp.float32), 'Wk': jax.random.normal(ks[2], (D, D), jnp.float32) * s, 'bk': jnp.zeros((D,), jnp.float32), 'Wv': jax.random.normal(ks[3], (D, D), jnp.float32) * s, 'bv': jnp.zeros((D,), jnp.float32), 'Wo': jax.random.normal(ks[4], (D, D), jnp.float32) * s, 'bo': jnp.zeros((D,), jnp.float32)}
    _L0_attn_a_in = _L0_attn_a_setup()

    def _L0_attn_b_setup():
        import jax, jax.numpy as jnp
        import numpy as np
        import math
        N_HEAD = 16

        def sparsemax_lastdim(z):
            z_sorted = jnp.flip(jnp.sort(z, axis=-1), axis=-1)
            cs = jnp.cumsum(z_sorted, axis=-1)
            d = z.shape[-1]
            rho = jnp.arange(1, d + 1, dtype=z.dtype)
            support = 1.0 + rho * z_sorted > cs
            k = jnp.maximum(jnp.sum(support, axis=-1, keepdims=True), 1)
            cs_k = jnp.take_along_axis(cs, k - 1, axis=-1)
            tau = (cs_k - 1.0) / k.astype(z.dtype)
            return jnp.maximum(z - tau, 0.0)
        key = jax.random.key(seed)
        k1, k2, k3, k4, k5 = jax.random.split(key, 5)
        B, T, C = (2, 256, 128)
        x = jax.random.normal(k1, (B, T, C), dtype=jnp.float32)
        w_attn = jax.random.normal(k2, (C, 3 * C), dtype=jnp.float32) * (1.0 / math.sqrt(C))
        b_attn = jax.random.normal(k3, (3 * C,), dtype=jnp.float32) * 0.02
        w_proj = jax.random.normal(k4, (C, C), dtype=jnp.float32) * (1.0 / math.sqrt(C))
        b_proj = jax.random.normal(k5, (C,), dtype=jnp.float32) * 0.02
        return {'x': x, 'w_attn': w_attn, 'b_attn': b_attn, 'w_proj': w_proj, 'b_proj': b_proj}
    _L0_attn_b_in = _L0_attn_b_setup()

    def _L0_ffn_setup():
        import jax, jax.numpy as jnp
        import numpy as np
        DIM = 128
        HIDDEN = 384
        SCALE = 1.0 / 127.0

        def _dequant(w_int, dtype):
            return w_int.astype(dtype) * jnp.asarray(SCALE, dtype)
        key = jax.random.key(seed)
        k_x, k_g, k_u, k_d = jax.random.split(key, 4)
        x = jax.random.normal(k_x, (4, 256, DIM), dtype=jnp.float32)
        w_gate = jax.random.randint(k_g, (HIDDEN, DIM), -127, 128, dtype=jnp.int32)
        w_up = jax.random.randint(k_u, (HIDDEN, DIM), -127, 128, dtype=jnp.int32)
        w_down = jax.random.randint(k_d, (DIM, HIDDEN), -127, 128, dtype=jnp.int32)
        return {'x': x, 'w_gate': w_gate, 'w_up': w_up, 'w_down': w_down}
    _L0_ffn_in = _L0_ffn_setup()
    _d = {'L0_attn_a_x': _L0_attn_a_in['x'], 'L0_attn_a_Wq': _L0_attn_a_in['Wq'], 'L0_attn_a_bq': _L0_attn_a_in['bq'], 'L0_attn_a_Wk': _L0_attn_a_in['Wk'], 'L0_attn_a_bk': _L0_attn_a_in['bk'], 'L0_attn_a_Wv': _L0_attn_a_in['Wv'], 'L0_attn_a_bv': _L0_attn_a_in['bv'], 'L0_attn_a_Wo': _L0_attn_a_in['Wo'], 'L0_attn_a_bo': _L0_attn_a_in['bo'], 'L0_attn_b_w_attn': _L0_attn_b_in['w_attn'], 'L0_attn_b_b_attn': _L0_attn_b_in['b_attn'], 'L0_attn_b_w_proj': _L0_attn_b_in['w_proj'], 'L0_attn_b_b_proj': _L0_attn_b_in['b_proj'], 'L0_ffn_w_gate': _L0_ffn_in['w_gate'], 'L0_ffn_w_up': _L0_ffn_in['w_up'], 'L0_ffn_w_down': _L0_ffn_in['w_down']}
    _x0 = _d['L0_attn_a_x']
    _d['L0_attn_a_x'] = jax.random.normal(jax.random.fold_in(jax.random.key(seed), 1), (16, 256, 128), dtype=_x0.dtype)
    del _x0
    return _d

def reference(L0_attn_a_x, L0_attn_a_Wq, L0_attn_a_bq, L0_attn_a_Wk, L0_attn_a_bk, L0_attn_a_Wv, L0_attn_a_bv, L0_attn_a_Wo, L0_attn_a_bo, L0_attn_b_w_attn, L0_attn_b_b_attn, L0_attn_b_w_proj, L0_attn_b_b_proj, L0_ffn_w_gate, L0_ffn_w_up, L0_ffn_w_down):

    def _L0_attn_a_ref(x, Wq, bq, Wk, bk, Wv, bv, Wo, bo):
        import jax, jax.numpy as jnp
        import numpy as np
        B, T, D, H = (4, 256, 128, 16)
        HD = D // H
        ROPE_BASE = 10000.0

        def rotate_half(x):
            x1 = x[..., ::2]
            x2 = x[..., 1::2]
            return jnp.stack((-x2, x1), axis=-1).reshape(x.shape)

        def rope_tables(seq_len, dim, dtype=jnp.float32):
            inv = 1.0 / ROPE_BASE ** (jnp.arange(0, dim, 2, dtype=jnp.float32) / dim)
            t = jnp.arange(seq_len, dtype=jnp.float32)
            freqs = jnp.einsum('i,j->ij', t, inv)
            emb = jnp.concatenate((freqs, freqs), axis=-1)
            return (jnp.cos(emb).astype(dtype)[None, None], jnp.sin(emb).astype(dtype)[None, None])
        b, t, d = x.shape

        def proj(W, bias):
            return (x @ W.T + bias).reshape(b, t, H, HD).transpose(0, 2, 1, 3)
        q, k, v = (proj(Wq, bq), proj(Wk, bk), proj(Wv, bv))
        cos, sin = rope_tables(t, HD, x.dtype)
        q = q * cos + rotate_half(q) * sin
        k = k * cos + rotate_half(k) * sin
        scale = 1.0 / jnp.sqrt(jnp.asarray(HD, x.dtype))
        attn = jnp.einsum('bhqd,bhkd->bhqk', q, k) * scale
        attn = jax.nn.softmax(attn, axis=-1)
        out = jnp.einsum('bhqk,bhkd->bhqd', attn, v)
        out = out.transpose(0, 2, 1, 3).reshape(b, t, d)
        return out @ Wo.T + bo

    def _L0_attn_b_ref(x, w_attn, b_attn, w_proj, b_proj):
        import jax, jax.numpy as jnp
        import numpy as np
        import math
        N_HEAD = 16

        def sparsemax_lastdim(z):
            z_sorted = jnp.flip(jnp.sort(z, axis=-1), axis=-1)
            cs = jnp.cumsum(z_sorted, axis=-1)
            d = z.shape[-1]
            rho = jnp.arange(1, d + 1, dtype=z.dtype)
            support = 1.0 + rho * z_sorted > cs
            k = jnp.maximum(jnp.sum(support, axis=-1, keepdims=True), 1)
            cs_k = jnp.take_along_axis(cs, k - 1, axis=-1)
            tau = (cs_k - 1.0) / k.astype(z.dtype)
            return jnp.maximum(z - tau, 0.0)
        B, T, C = x.shape
        H = N_HEAD
        hd = C // H
        qkv = x @ w_attn + b_attn
        q, k, v = jnp.split(qkv, 3, axis=-1)
        q = q.reshape(B, T, H, hd).transpose(0, 2, 1, 3)
        k = k.reshape(B, T, H, hd).transpose(0, 2, 1, 3)
        v = v.reshape(B, T, H, hd).transpose(0, 2, 1, 3)
        att = jnp.einsum('bhqd,bhkd->bhqk', q, k) * (1.0 / math.sqrt(hd))
        causal = jnp.tril(jnp.ones((T, T), dtype=bool))
        att = jnp.where(causal[None, None], att, -jnp.inf)
        att = sparsemax_lastdim(att)
        y = jnp.einsum('bhqk,bhkd->bhqd', att, v)
        y = y.transpose(0, 2, 1, 3).reshape(B, T, C)
        return y @ w_proj + b_proj

    def _L0_ffn_ref(x, w_gate, w_up, w_down):
        import jax, jax.numpy as jnp
        import numpy as np
        DIM = 128
        HIDDEN = 384
        SCALE = 1.0 / 127.0

        def _dequant(w_int, dtype):
            return w_int.astype(dtype) * jnp.asarray(SCALE, dtype)
        wg = _dequant(w_gate, x.dtype)
        wu = _dequant(w_up, x.dtype)
        wd = _dequant(w_down, x.dtype)
        gate = jnp.einsum('bsd,hd->bsh', x, wg)
        up = jnp.einsum('bsd,hd->bsh', x, wu)
        h = jax.nn.silu(gate) * up
        return jnp.einsum('bsh,dh->bsd', h, wd)
    x = L0_attn_a_x
    x = x + _L0_attn_a_ref(_layernorm(x, axis=-1), L0_attn_a_Wq, L0_attn_a_bq, L0_attn_a_Wk, L0_attn_a_bk, L0_attn_a_Wv, L0_attn_a_bv, L0_attn_a_Wo, L0_attn_a_bo)
    x = x + _L0_ffn_ref(_layernorm(x, axis=-1), L0_ffn_w_gate, L0_ffn_w_up, L0_ffn_w_down)
    x = x + _L0_attn_b_ref(_layernorm(x, axis=-1), L0_attn_b_w_attn, L0_attn_b_b_attn, L0_attn_b_w_proj, L0_attn_b_b_proj)
    x = x + _L0_ffn_ref(_layernorm(x, axis=-1), L0_ffn_w_gate, L0_ffn_w_up, L0_ffn_w_down)
    return x

_drawn_inputs = setup_inputs


def setup_inputs(seed=0):
    import zlib

    import numpy as np

    out = dict(_drawn_inputs(seed))
    spreads = {'L0_attn_a_bq': (0.0, 0.8),
     'L0_attn_a_bk': (0.0, 0.8),
     'L0_attn_a_bv': (0.0, 0.1),
     'L0_attn_a_bo': (0.0, 0.1)}
    factors = {'L0_attn_a_Wq': 8.0,
     'L0_attn_a_Wk': 8.0,
     'L0_attn_a_Wv': 8.0,
     'L0_attn_b_w_attn': 8.0,
     'L0_attn_b_b_attn': 8.0,
     'L0_attn_b_w_proj': 8.0,
     'L0_attn_b_b_proj': 8.0}
    for name, (base, spread) in spreads.items():
        noise = np.random.default_rng([zlib.crc32(name.encode()), seed]).standard_normal(out[name].shape)
        drawn = base * np.exp(spread * noise) if base else spread * noise
        out[name] = jnp.asarray(drawn.astype(out[name].dtype))
    for name, factor in factors.items():
        out[name] = (out[name] * factor).astype(out[name].dtype)
    return out
```

```python
from contextlib import ExitStack

import concourse.bass as bass
from concourse import mybir
import numpy as np

F32 = mybir.dt.float32
BF16 = mybir.dt.bfloat16
I32 = mybir.dt.int32
ALU = mybir.AluOpType
ACT = mybir.ActivationFunctionType
AX = mybir.AxisListType

B, T, D, H = 16, 256, 128, 16
HD = D // H
P = 128
TT = T // P
HIDDEN = 384
NC_H = HIDDEN // P
EPS = 1e-5
SCALE = float(np.float32(1.0) / np.sqrt(np.float32(HD)))
STACKS = 3
PARTS = 3
STACK = PARTS * PARTS * HD
NEG = -1.0e30
BISECTIONS = 28
Q = 4
SEM = 16

WA = dict(q=0, qs=128, k=256, ks=384, v=512, o=640, bq=768, bqs=769, bk=770, bks=771, bv=772, bo=900)
WA_COLS = 1028
WB = dict(q=0, k=128, v=256, o=384, bq=512, bk=513, bv=514, bo=642)
WB_COLS = 770
CC = dict(ident=0, cos=128, sin=384, mask=640, maskT=768, invk=896, seg=1152)
CC_COLS = 1408


class Places:
    pass


def allocate(nc, ctx):
    m = Places()

    def sb(name, shape, dt=F32):
        return ctx.enter_context(nc.sbuf_tensor(name, shape, dt))

    m.x = sb("x", [P, (B + 1) * TT, D])
    m.x2 = sb("x2", [P, B * TT, D])
    m.wa = sb("wa", [P, WA_COLS])
    m.wb = sb("wb", [P, WB_COLS])
    m.wf_int = sb("wf_int", [P, 3 * HIDDEN], I32)
    m.wf = sb("wf", [P, 3 * HIDDEN])
    m.cc = sb("cc", [P, CC_COLS])
    m.ident_b = sb("ident_b", [P, P], BF16)
    m.mask_b = sb("mask_b", [P, P], BF16)
    m.maskT_b = sb("maskT_b", [P, P], BF16)
    m.neghalf = sb("neghalf", [P, 4])
    m.zero_rows = sb("zero_rows", [PARTS * H, T], BF16)
    m.one_rows = sb("one_rows", [PARTS * H, T], BF16)
    m.qs = [sb(f"q_stack{r}", [P, H, T], BF16) for r in range(STACKS)]
    m.ks = [sb(f"k_stack{r}", [P, H, T], BF16) for r in range(STACKS)]
    m.v = [sb(f"v_ext{r}", [P, TT, H, 32]) for r in range(STACKS)]
    m.pt = sb("probs_t", [P, 2, Q, 2 * T])
    m.stats = sb("bn_out", [P, 4, 6])
    m.mv = sb("mean_var", [P, 4, 2])
    m.ve = sb("var_eps", [P, 4])
    m.rstd = sb("rstd", [P, 4])
    m.xhat = sb("xhat", [P, 4, D])
    m.xT = sb("xT", [P, 2, 512])
    m.tc = sb("rope_cos_terms", [P, 2, T])
    m.ts = sb("rope_sin_terms", [P, 2, T])
    m.qk = sb("qk", [P, 2, T])
    m.parts = sb("qk_parts", [P, PARTS, 2, T], BF16)
    m.nm = sb("neg_shift", [P, STACKS, H, TT])
    m.nm_rest = sb("neg_shift_rest", [P, H, TT])
    m.nm_parts = sb("neg_shift_parts", [P, TT, PARTS, H], BF16)
    m.nmT = sb("neg_shift_rows", [PARTS * H, T], BF16)
    m.ot = sb("out_t", [P, Q, T])
    m.oc = sb("out_compact", [P, T])
    m.den = sb("denominators", [P, T])
    m.rden = sb("rdenominators", [P, T])
    m.ocn = sb("out_normal", [P, T])
    m.xb = sb("x_plus_bias", [P, TT, D])
    m.z8 = sb("top8", [P, H, TT, 8])
    m.cs = sb("top8_sums", [P, H, TT, 8])
    m.excess = sb("excess", [P, H, TT])
    m.worst = sb("worst", [P, H, TT])
    m.flag = sb("flag", [P, 1])
    m.redo = sb("redo", [1, 1], I32)
    m.z_max, m.low, m.width, m.mid, m.z_sum = (sb(n, [P, TT]) for n in ("z_max", "low", "width", "mid", "z_sum"))
    m.z_rows = sb("z_rows", [P, TT, T])
    m.z_work = sb("z_work", [P, TT, T])
    m.silu = sb("silu", [P, 2, 512])
    m.hid = sb("hidden", [P, 2, NC_H, 512])
    m.banks = ctx.enter_context(nc.psum_tensor("banks", [P, 8, 512], F32))
    m.passed = {e.engine: ctx.enter_context(nc.semaphore(f"passed_{n}"))
                for n, e in (("sp", nc.sync), ("pool", nc.gpsimd), ("dve", nc.vector), ("pe", nc.tensor))}
    return m


def wait_apart(m, eng, s, value):
    if not isinstance(value, int):
        eng.wait_ge(s, value)
        eng.sem_inc(m.passed[eng.engine], 1)
    elif value > 0:
        eng.wait_ge(s, value)


def setup_phase(nc, ctx, m, io):
    def sem(name):
        return ctx.enter_context(nc.semaphore(name))

    loaded_a = sem("loaded_a")
    loaded_b = sem("loaded_b")
    zeroed = sem("zeroed")
    ones_set = sem("ones_set")
    ones_rows = sem("ones_rows")
    x_loaded = sem("x_loaded")
    consts = sem("consts_ready")
    x_d = io["x"].rearrange("b (t p) d -> p (b t) d", p=P)

    with nc.Block() as block:
        @block.sync
        def _(sp):
            sp.dma_start(m.x[:, 0:TT, :], x_d[:, 0:TT, :]).then_inc(x_loaded, SEM)
            sp.dma_start(m.cc[:, :], io["consts"]).then_inc(loaded_a, SEM)
            sp.dma_start(m.wa[:, :], io["wa"]).then_inc(loaded_a, SEM)
            sp.dma_start(m.x[:, TT:B * TT, :], x_d[:, TT:B * TT, :]).then_inc(x_loaded, SEM)
            sp.dma_start(m.wf_int[:, :], io["wf"]).then_inc(loaded_b, SEM)
            sp.dma_start(m.wb[:, :], io["wb"]).then_inc(loaded_b, SEM)
            sp.wait_ge(ones_set, 1)
            sp.wait_ge(zeroed, 2 * STACKS)
            for r in range(STACKS):
                sp.dma_start(m.ks[r][STACK:STACK + PARTS, :, :], m.one_rows[:, :]).then_inc(ones_rows, SEM)
            sp.wait_ge(ones_rows, STACKS * SEM)
            sp.wait_ge(x_loaded, 2 * SEM)
            sp.wait_ge(loaded_b, 2 * SEM)

        @block.gpsimd
        def _(pool):
            pool.memset(m.one_rows[:, :], 1.0).then_inc(ones_set, 1)
            pool.memset(m.neghalf[:, :], -0.5).then_inc(consts, 1)
            for r in range(STACKS):
                pool.memset(m.qs[r][:, :, :].bitcast(F32), 0.0).then_inc(zeroed, 1)

        @block.vector
        def _(dve):
            for r in range(STACKS):
                dve.memset(m.ks[r][:, :, :].bitcast(F32), 0.0).then_inc(zeroed, 1)
            dve.memset(m.x[:, B * TT:, :], 0.0).then_inc(consts, 1)
            dve.memset(m.worst[:, :, :], -1.0).then_inc(consts, 1)
            dve.memset(m.zero_rows[:, :], 0.0).then_inc(consts, 1)
            for r in range(STACKS):
                dve.memset(m.v[r][:, :, :, 0:8], 0.0).then_inc(consts, 1)
                dve.memset(m.v[r][:, :, :, 8:16], 1.0).then_inc(consts, 1)
                dve.memset(m.v[r][:, :, :, 16:32], 0.0).then_inc(consts, 1)
            dve.wait_ge(loaded_a, 2 * SEM)
            dve.tensor_copy(m.ident_b[:, :], m.cc[:, CC["ident"]:CC["ident"] + P]).then_inc(consts, 1)
            dve.tensor_copy(m.mask_b[:, :], m.cc[:, CC["mask"]:CC["mask"] + P]).then_inc(consts, 1)
            dve.tensor_copy(m.maskT_b[:, :], m.cc[:, CC["maskT"]:CC["maskT"] + P]).then_inc(consts, 1)
            dve.wait_ge(loaded_b, 2 * SEM)
            dve.tensor_scalar(m.wf[:, :], m.wf_int[:, :], float(np.float32(1.0 / 127.0)), None,
                              ALU.mult).then_inc(consts, 1)


def attention_phase(nc, ctx, m, io, kind, x_in, x_out):
    soft = kind == "a"
    general = kind == "g"
    w, at = (m.wa, WA) if soft else (m.wb, WB)

    def sem(name):
        return ctx.enter_context(nc.semaphore(f"{kind}_{name}"))

    ln_stats = sem("ln_stats")
    var_ready = sem("var_ready")
    eps_added = sem("eps_added")
    rstd_ready = sem("rstd_ready")
    xhat_ready = sem("xhat_ready")
    dense_full = sem("dense_full")
    dense_free = sem("dense_free")
    qk_step = sem("qk_step")
    qk_split = sem("qk_split")
    image_stored = sem("image_stored")
    stack_loaded = sem("stack_loaded")
    v_ready = sem("v_ready")
    scores_ready = sem("scores_ready")
    reduced = sem("reduced")
    shift_step = sem("shift_step")
    shift_split = sem("shift_split")
    shift_rows = sem("shift_rows")
    shifted_ready = sem("shifted_ready")
    probs_ready = sem("probs_ready")
    pv_done = sem("pv_done")
    ot_ready = sem("ot_ready")
    ot_stored = sem("ot_stored")
    oc_loaded = sem("oc_loaded")
    rden_ready = sem("rden_ready")
    ocn_ready = sem("ocn_ready")
    xb_ready = sem("xb_ready")
    tau_step = sem("tau_step")

    q_image = nc.dram_tensor(f"{kind}_q_image", [5, P, T], BF16, kind="Internal").ap()
    k_image = nc.dram_tensor(f"{kind}_k_image", [PARTS, P, T], BF16, kind="Internal").ap()
    o_image = nc.dram_tensor(f"{kind}_o_image", [Q, 32, Q, T], F32, kind="Internal").ap()
    q_rows = q_image.rearrange("s (d h) t -> (s d) h t", h=H)
    k_rows = k_image.rearrange("s (d h) t -> (s d) h t", h=H)
    o_rows = o_image.rearrange("i d g t -> i (d g) t")

    ident = m.cc[:, CC["ident"]:CC["ident"] + P]
    score_banks = m.banks[:, 0:2, :]
    shifted_banks = m.banks[:, 2:6, :]
    out_bank = m.banks[:, 6, :]
    dense = m.banks[:, 7, :]
    dense_b = m.banks[:, 7:8, :].bitcast(BF16)

    if general:
        USES = [("xT", 0), ("q", 0), ("v", 0), ("shift", 0), ("proj", 0)]
        FIRST = 1
        RING = 1
    else:
        USES = [("xT", 0), ("q", 0), ("shift", 2)] + ([("k", 0)] if soft else []) + [("proj", 4), ("v", 0)]
        FIRST = 4
        RING = STACKS
    OUT = dict(USES)["proj"]
    SLOTS = B + OUT

    def live(t, lag):
        return not isinstance(t, int) or 0 <= t - lag < B

    def uses_before(t, use):
        inside = [n for n, _ in USES].index(use)
        if isinstance(t, int):
            return (sum(live(s, lag) for s in range(t) for _, lag in USES)
                    + sum(live(t, lag) for _, lag in USES[:inside]))
        first = sum(live(s, lag) for s in range(FIRST) for _, lag in USES)
        return (t - FIRST) * len(USES) + (first + inside)

    def sums_done(t):
        return uses_before(t, "proj") + 1 if live(t, OUT) else 0

    def wait(eng, s, value):
        if not isinstance(value, int) or value > 0:
            eng.wait_ge(s, value)

    def run_slots(eng, slot):
        turns = (B - FIRST) // RING
        for t in range(FIRST):
            slot(t, t % RING)
        with eng.Fori(0, turns) as n:
            for k in range(RING):
                slot(n * RING + (FIRST + k), (FIRST + k) % RING)
        for t in range(FIRST + turns * RING, SLOTS):
            slot(t, t % RING)

    def run_batches(eng, batch):
        redo = eng.value_load(m.redo[0:1, 0:1], min_val=0, max_val=1)
        with eng.If(redo > 0):
            run_slots(eng, lambda b, r: batch(b))

    def pair_of(j):
        return (j - 4) % 8, (2 if j >= 4 else 3)

    with nc.Block() as block:

        @block.sync
        def _(sp):
            def store_image(b):
                wait_apart(m, sp, qk_split, b + 1)
                wait(sp, stack_loaded, b * (7 * SEM))
                sp.dma_start(q_image[0:3].rearrange("s p t -> p s t"), m.parts[:, :, 0, :]).then_inc(image_stored, SEM)
                sp.dma_start(k_image.rearrange("s p t -> p s t"), m.parts[:, :, 1, :]).then_inc(image_stored, SEM)
                sp.dma_start(q_image[3:5].rearrange("s p t -> p s t"), m.parts[:, 0:2, 0, :]).then_inc(image_stored, SEM)

            def load_stack(b, r):
                wait_apart(m, sp, image_stored, (b + 1) * (3 * SEM))
                wait(sp, shifted_ready, (b - (RING - 1)) * 8)
                sp.dma_start(m.qs[r][STACK:STACK + PARTS, :, :], m.zero_rows[:, :]).then_inc(stack_loaded, SEM)
                for rep in range(PARTS):
                    rows = slice(rep * PARTS * HD, (rep + 1) * PARTS * HD)
                    sp.dma_start(m.qs[r][rows, :, :], q_rows[rep * HD:(rep + PARTS) * HD]).then_inc(stack_loaded, SEM)
                    sp.dma_start(m.ks[r][rows, :, :], k_rows[0:PARTS * HD]).then_inc(stack_loaded, SEM)

            def load_shift(b, t, r):
                wait_apart(m, sp, dense_free, uses_before(t, "shift") + 1)
                sp.dma_start(m.qs[r][STACK:STACK + PARTS, :, :], m.nmT[:, :]).then_inc(shift_rows, SEM)

            def store_out(b):
                wait_apart(m, sp, ot_ready, b * 2 + 2)
                wait(sp, oc_loaded, b * ((2 if soft else 1) * SEM))
                sp.dma_start(o_image.rearrange("i d g t -> (i d) g t"), m.ot[:, :, :]).then_inc(ot_stored, SEM)

            def load_out(b, t):
                wait_apart(m, sp, ot_stored, (b + 1) * SEM)
                if soft:
                    wait(sp, ocn_ready, b)
                else:
                    wait(sp, dense_free, sums_done(t - 1 if general else t))
                sp.dma_start(m.oc[:, :], o_rows[:, 0:HD * Q, :]).then_inc(oc_loaded, SEM)
                if soft:
                    sp.dma_start(m.den[:, :], o_rows[:, HD * Q:2 * HD * Q, :]).then_inc(oc_loaded, SEM)

            def slot(t, r):
                if live(t, 2):
                    load_shift(t - 2, t, (r - 2) % RING)
                if live(t, 0):
                    store_image(t)
                if live(t, 3):
                    store_out(t - 3)
                if live(t, 0):
                    load_stack(t, r)
                if live(t, 3):
                    load_out(t - 3, t)

            def batch(b):
                store_image(b)
                load_stack(b, 0)
                load_shift(b, b, 0)
                store_out(b)
                load_out(b, b)

            if general:
                run_batches(sp, batch)
            else:
                run_slots(sp, slot)

        @block.gpsimd
        def _(pool):
            def rstd(b):
                wait_apart(m, pool, var_ready, b * 2 + 2)
                pool.tensor_scalar(m.ve[:, 0:TT], m.mv[:, 0:TT, 1], EPS, None, ALU.add).then_inc(eps_added, 1)
                pool.wait_ge(eps_added, b + 1)
                wait(pool, xhat_ready, b * 2)
                pool.tensor_tensor(m.rstd[:, 0:TT], m.ve[:, 0:TT], m.neghalf[:, 0:TT], ALU.pow).then_inc(rstd_ready, 1)

            def split_shift(b, r):
                if soft or general:
                    pool.wait_ge(reduced, (b + 1) * H)
                else:
                    pool.wait_ge(tau_step, b * 5 + 3)
                wait_apart(m, pool, shift_rows, b * SEM)
                nm = m.nm[:, r, :, :]
                out = [m.nm_parts[:, :, n, :].rearrange("p q h -> p h q") for n in range(PARTS)]
                pool.tensor_copy(out[0], nm).then_inc(shift_step, 1)
                pool.wait_ge(shift_step, b * 3 + 1)
                pool.tensor_tensor(m.nm_rest[:, :, :], nm, out[0], ALU.subtract).then_inc(shift_step, 1)
                wait_apart(m, pool, shift_step, b * 3 + 2)
                pool.tensor_copy(out[1], m.nm_rest[:, :, :]).then_inc(shift_step, 1)
                pool.wait_ge(shift_step, b * 3 + 3)
                pool.tensor_tensor(out[2], m.nm_rest[:, :, :], out[1], ALU.subtract).then_inc(shift_split, 1)

            def split_qk(b, t):
                pool.wait_ge(dense_free, uses_before(t, "k" if soft else "q") + 1)
                if soft:
                    pool.tensor_tensor(m.qk[:, :, :], m.tc[:, :, :], m.ts[:, :, :], ALU.add).then_inc(qk_step, 1)
                    pool.wait_ge(qk_step, b * 4 + 1)
                n = 1 if soft else 0
                per = 4 if soft else 3
                wait_apart(m, pool, image_stored, b * (3 * SEM))
                pool.tensor_copy(m.parts[:, 0, :, :], m.qk[:, :, :]).then_inc(qk_step, 1)
                pool.wait_ge(qk_step, b * per + n + 1)
                pool.tensor_tensor(m.qk[:, :, :], m.qk[:, :, :], m.parts[:, 0, :, :], ALU.subtract).then_inc(qk_step, 1)
                wait_apart(m, pool, qk_step, b * per + n + 2)
                pool.tensor_copy(m.parts[:, 1, :, :], m.qk[:, :, :]).then_inc(qk_step, 1)
                pool.wait_ge(qk_step, b * per + n + 3)
                pool.tensor_tensor(m.parts[:, 2, :, :], m.qk[:, :, :], m.parts[:, 1, :, :], ALU.subtract).then_inc(qk_split, 1)

            def add_bias(b, t):
                wait(pool, dense_free, sums_done(t - 1))
                for tt in range(TT):
                    pool.tensor_tensor(m.xb[:, tt, :], x_in[:, bass.ds(b * TT + tt, 1), :].rearrange("p o d -> p (o d)"), w[:, at["bo"]:at["bo"] + D],
                                       ALU.add).then_inc(xb_ready, 1)

            def slot(t, r):
                if live(t, 2):
                    split_shift(t - 2, (r - 2) % RING)
                if live(t, -1):
                    rstd(t + 1)
                if live(t, OUT):
                    add_bias(t - OUT, t)
                if live(t, 0):
                    split_qk(t, t)

            def batch(b):
                rstd(b)
                split_qk(b, b)
                split_shift(b, 0)
                add_bias(b, b)

            if general:
                run_batches(pool, batch)
            else:
                rstd(0)
                run_slots(pool, slot)

        @block.vector
        def _(dve):
            def layernorm_stats(b):
                wait(dve, xhat_ready, b * 2)
                for tt in range(TT):
                    dve.bn_stats(m.stats[:, tt, :], x_in[:, bass.ds(b * TT + tt, 1), :].rearrange("p o d -> p (o d)")).then_inc(ln_stats, 1)
                wait_apart(m, dve, ln_stats, b * 2 + 2)
                for tt in range(TT):
                    dve.bn_aggr(m.mv[:, tt, :], m.stats[:, tt, :]).then_inc(var_ready, 1)

            def layernorm_apply(b, t):
                dve.wait_ge(rstd_ready, b + 1)
                if isinstance(b, int) and b == 0:
                    pass
                else:
                    dve.wait_ge(dense_full, uses_before(t, "xT") + 1)
                for tt in range(TT):
                    dve.tensor_scalar(m.xhat[:, tt, :], x_in[:, bass.ds(b * TT + tt, 1), :].rearrange("p o d -> p (o d)"), m.mv[:, tt, 0:1],
                                      m.rstd[:, tt:tt + 1], ALU.subtract, ALU.mult).then_inc(xhat_ready, 1)

            def rope(b, t, n, use):
                wait(dve, qk_split, b)
                dve.wait_ge(dense_full, uses_before(t, use) + 1)
                bias, bias_s = at["b" + use], at["b" + use + "s"]
                dve.scalar_tensor_tensor(m.tc[:, n, :], dense[:, 0:T], w[:, bias:bias + 1],
                                         m.cc[:, CC["cos"]:CC["cos"] + T], ALU.add, ALU.mult)
                dve.scalar_tensor_tensor(m.ts[:, n, :], dense[:, T:2 * T], w[:, bias_s:bias_s + 1],
                                         m.cc[:, CC["sin"]:CC["sin"] + T], ALU.add, ALU.mult).then_inc(dense_free, 1)

            def take_qk(b, t):
                wait(dve, qk_split, b)
                dve.wait_ge(dense_full, uses_before(t, "q") + 1)
                dve.tensor_scalar(m.qk[:, 0, :], dense[:, 0:T], w[:, at["bq"]:at["bq"] + 1], SCALE, ALU.add, ALU.mult)
                dve.tensor_scalar(m.qk[:, 1, :], dense[:, T:2 * T], w[:, at["bk"]:at["bk"] + 1], None,
                                  ALU.add).then_inc(dense_free, 1)

            def take_v(b, t, r):
                wait(dve, pv_done, (b - (RING - 1)) * 4)
                dve.wait_ge(dense_full, uses_before(t, "v") + 1)
                bv = w[:, at["bv"]:at["bv"] + D].rearrange("p (h d) -> p h d", d=HD)
                for tt in range(TT):
                    ins = dve.tensor_tensor(m.v[r][:, tt, :, 0:HD],
                                            dense[:, tt * D:(tt + 1) * D].rearrange("p (h d) -> p h d", d=HD),
                                            bv, ALU.add)
                    if tt == TT - 1:
                        ins.then_inc(dense_free, 1)

            def reduce_head(b, r, h):
                wait_apart(m, dve, scores_ready, b * H + (h + 1))
                bank = score_banks[:, h % 2, :]
                if soft:
                    dve.tensor_reduce(m.nm[:, r, h, :], bank.rearrange("p (q k) -> p q k", q=TT), AX.X, ALU.max,
                                      negate=True).then_inc(reduced, 1)
                else:
                    dve.max(m.z8[:, h, 0, :], bank[:, 0:P])
                    dve.max(m.z8[:, h, 1, :], bank[:, P:P + T]).then_inc(reduced, 1)

            def tau(b, r):
                z = m.z8[:, :, :, :].rearrange("p h q k -> p (h q k)")
                cs = m.cs[:, :, :, :].rearrange("p h q k -> p (h q k)")
                c = m.cs[:, :, :, :].rearrange("p h q k -> p (h q) k")
                dve.wait_ge(reduced, (b + 1) * H)
                dve.tensor_tensor_scan(cs, m.cc[:, CC["seg"]:CC["seg"] + 256], z, 0.0, ALU.mult,
                                       ALU.add).then_inc(tau_step, 1)
                dve.wait_ge(tau_step, b * 5 + 1)
                dve.scalar_tensor_tensor(cs, cs, -1.0, m.cc[:, CC["invk"]:CC["invk"] + 256], ALU.add,
                                         ALU.mult).then_inc(tau_step, 1)
                dve.wait_ge(tau_step, b * 5 + 2)
                dve.tensor_reduce(m.nm[:, r, :, :].rearrange("p h q -> p (h q)"), c, AX.X, ALU.max,
                                  negate=True).then_inc(tau_step, 1)
                dve.wait_ge(tau_step, b * 5 + 3)
                dve.tensor_tensor(m.excess[:, :, :], m.z8[:, :, :, 7], m.nm[:, r, :, :], ALU.add).then_inc(tau_step, 1)
                dve.wait_ge(tau_step, b * 5 + 4)
                dve.tensor_tensor(m.worst[:, :, :], m.worst[:, :, :], m.excess[:, :, :], ALU.max).then_inc(tau_step, 1)

            def bisect_head(b, h):
                wait_apart(m, dve, scores_ready, b * H + (h + 1))
                bank = score_banks[:, h % 2, :]
                rows = (bank[:, 0:P], bank[:, P:P + T])
                z = (m.z_rows[:, 0, 0:P], m.z_rows[:, 1, :])
                for q in range(TT):
                    dve.tensor_reduce(m.z_max[:, q:q + 1], rows[q], AX.X, ALU.max)
                dve.memset(m.z_rows[:, 0, P:T], NEG)
                dve.memset(m.low[:, :], -1.0)
                dve.memset(m.width[:, :], 0.5)
                dve.drain()
                for q in range(TT):
                    ins = dve.tensor_scalar(z[q], rows[q], m.z_max[:, q:q + 1], None, ALU.subtract)
                dve.drain()
                with dve.Fori(0, BISECTIONS):
                    dve.tensor_tensor(m.mid[:, :], m.low[:, :], m.width[:, :], ALU.add)
                    dve.drain()
                    for q in range(TT):
                        dve.tensor_scalar(m.z_work[:, q, :], m.z_rows[:, q, :], m.mid[:, q:q + 1], 0.0,
                                          ALU.subtract, ALU.max)
                    dve.drain()
                    dve.tensor_reduce(m.z_sum[:, :], m.z_work[:, :, :], AX.X, ALU.add)
                    dve.drain()
                    dve.tensor_scalar(m.z_sum[:, :], m.z_sum[:, :], 1.0, None, ALU.is_ge)
                    dve.drain()
                    dve.tensor_tensor(m.z_sum[:, :], m.z_sum[:, :], m.width[:, :], ALU.mult)
                    dve.drain()
                    dve.tensor_tensor(m.low[:, :], m.low[:, :], m.z_sum[:, :], ALU.add)
                    dve.tensor_scalar(m.width[:, :], m.width[:, :], 0.5, None, ALU.mult)
                    dve.drain()
                for q in range(TT):
                    dve.tensor_scalar(m.z_work[:, q, :], m.z_rows[:, q, :], m.low[:, q:q + 1], None, ALU.is_gt)
                dve.drain()
                dve.tensor_reduce(m.mid[:, :], m.z_work[:, :, :], AX.X, ALU.add)
                dve.drain()
                dve.tensor_tensor(m.z_work[:, :, :], m.z_work[:, :, :], m.z_rows[:, :, :], ALU.mult)
                dve.drain()
                dve.tensor_reduce(m.z_sum[:, :], m.z_work[:, :, :], AX.X, ALU.add)
                dve.reciprocal(m.mid[:, :], m.mid[:, :])
                dve.drain()
                dve.scalar_tensor_tensor(m.z_sum[:, :], m.z_sum[:, :], -1.0, m.mid[:, :], ALU.add, ALU.mult)
                dve.drain()
                dve.tensor_tensor(m.z_sum[:, :], m.z_sum[:, :], m.z_max[:, :], ALU.add)
                dve.drain()
                if h == 0:
                    wait(dve, shift_split, b)
                dve.tensor_scalar(m.nm[:, 0, h, :], m.z_sum[:, :], -1.0, None, ALU.mult).then_inc(reduced, 1)

            def normalise(b, t):
                wait(dve, dense_full, sums_done(t - 1))
                dve.wait_ge(oc_loaded, (b + 1) * (2 * SEM))
                dve.reciprocal(m.rden[:, :], m.den[:, :]).then_inc(rden_ready, 1)
                dve.wait_ge(rden_ready, b + 1)
                dve.tensor_tensor(m.ocn[:, :], m.oc[:, :], m.rden[:, :], ALU.mult).then_inc(ocn_ready, 1)

            def residual(b, t):
                dve.wait_ge(dense_full, uses_before(t, "proj") + 1)
                dve.wait_ge(xb_ready, b * 2 + 2)
                dve.tensor_tensor(x_out[:, bass.ds(b * TT, TT), :], dense[:, 0:TT * D].rearrange("p (q d) -> p q d", q=TT),
                                  m.xb[:, :, :], ALU.add).then_inc(dense_free, 1)

            def slot(t, r):
                for h in range(H):
                    if h == 0 and live(t, -1):
                        layernorm_stats(t + 1)
                    if live(t, 1):
                        reduce_head(t - 1, (r - 1) % RING, h)
                    if live(t, 0):
                        if h == 1:
                            rope(t, t, 0, "q") if soft else take_qk(t, t)
                        if h == 3 and soft:
                            rope(t, t, 1, "k")
                        if h == 11:
                            take_v(t, t, r)
                    if h == 6 and live(t, -1):
                        layernorm_apply(t + 1, t)
                    if h == 1 and live(t, OUT) and soft:
                        normalise(t - OUT, t)
                    if h == 6 and live(t, OUT):
                        residual(t - OUT, t)
                if live(t, 1) and not soft:
                    tau(t - 1, (r - 1) % RING)

            def batch(b):
                layernorm_stats(b)
                layernorm_apply(b, b - 1)
                take_qk(b, b)
                take_v(b, b, 0)
                for h in range(H):
                    bisect_head(b, h)
                residual(b, b)

            if general:
                run_batches(dve, batch)
            else:
                layernorm_stats(0)
                layernorm_apply(0, 0)
                run_slots(dve, slot)

        @block.scalar
        def _(act):
            def take_xT(t):
                act.wait_ge(dense_full, uses_before(t, "xT") + 1)
                act.copy(m.xT[:, 0, 0:T], dense[:, 0:T]).then_inc(dense_free, 1)

            def take_shift(b, t):
                wait(act, shift_rows, b * SEM)
                act.wait_ge(dense_full, uses_before(t, "shift") + 1)
                act.copy(m.nmT[:, :], dense_b[0:PARTS * H, 0, 0:T]).then_inc(dense_free, 1)

            def probs(b, p):
                wait(act, pv_done, b * 4 + (p // 2 - 1))
                act.wait_ge(shifted_ready, b * 8 + (p + 1))
                n = 2 * T if soft else T + P
                act.activation(m.pt[:, (p // 2) % 2, 2 * (p % 2):2 * (p % 2) + 2, 0:n],
                               shifted_banks[:, 2 * (p % 2):2 * (p % 2) + 2, 0:n],
                               ACT.Exp if soft else ACT.Relu, scale=SCALE if soft else 1.0).then_inc(probs_ready, 1)

            def take_out(b, half):
                act.wait_ge(pv_done, b * 4 + (2 * half + 2))
                if half == 0:
                    wait(act, ot_stored, b * SEM)
                act.copy(m.ot[:, 2 * half:2 * half + 2, :],
                         out_bank.rearrange("p (g t) -> p g t", g=2)).then_inc(ot_ready, 1)

            def slot(t, r):
                if live(t, 0):
                    take_xT(t)
                for j in range(8):
                    p, lag = pair_of(j)
                    if j == 1 and live(t, 2):
                        take_shift(t - 2, t)
                    if live(t, lag):
                        probs(t - lag, p)
                    if p == 4 and live(t, lag):
                        take_out(t - lag, 0)
                    if p == 0 and live(t, lag + 1):
                        take_out(t - lag - 1, 1)

            def batch(b):
                take_xT(b)
                take_shift(b, b)
                for p in range(H // 2):
                    probs(b, p)
                    if p % 4 == 3:
                        take_out(b, p // 4)

            if general:
                run_batches(act, batch)
            else:
                run_slots(act, slot)

        @block.tensor
        def _(pe):
            def transpose_x(b, t):
                pe.wait_ge(xhat_ready, b * 2 + 2)
                wait(pe, dense_free, uses_before(t, "xT"))
                for tt in range(TT):
                    ins = pe.transpose(dense[:, tt * P:(tt + 1) * P], m.xhat[:, tt, :], ident)
                ins.then_inc(dense_full, 1)

            def project(t, use, names):
                pe.wait_ge(dense_free, uses_before(t, use))
                for n, name in enumerate(names):
                    ins = pe.matmul(dense[:, n * T:(n + 1) * T], w[:, at[name]:at[name] + P], m.xT[:, 0, 0:T],
                                    start=True, stop=True)
                ins.then_inc(dense_full, 1)

            def project_v(t):
                pe.wait_ge(dense_free, uses_before(t, "v"))
                for tt in range(TT):
                    ins = pe.matmul(dense[:, tt * D:(tt + 1) * D], m.xT[:, 0, tt * P:(tt + 1) * P],
                                    w[:, at["v"]:at["v"] + D], start=True, stop=True)
                ins.then_inc(dense_full, 1)

            def transpose_shift(b, t):
                pe.wait_ge(shift_split, b + 1)
                wait_apart(m, pe, dense_free, uses_before(t, "shift"))
                for qt in range(TT):
                    ins = pe.transpose(dense_b[0:PARTS * H, 0, qt * P:(qt + 1) * P],
                                       m.nm_parts[:, qt, :, :].rearrange("p s h -> p (s h)"), m.ident_b[:, :])
                ins.then_inc(dense_full, 1)

            def project_out(b, t):
                if soft:
                    pe.wait_ge(ocn_ready, b + 1)
                else:
                    pe.wait_ge(oc_loaded, (b + 1) * SEM)
                src = m.ocn if soft else m.oc
                pe.wait_ge(dense_free, uses_before(t, "proj"))
                for tt in range(TT):
                    ins = pe.matmul(dense[:, tt * D:(tt + 1) * D], src[:, tt * P:(tt + 1) * P],
                                    w[:, at["o"]:at["o"] + D], start=True, stop=True)
                ins.then_inc(dense_full, 1)

            def pass1(b, r, h):
                if h == 0:
                    pe.wait_ge(stack_loaded, (b + 1) * (7 * SEM))
                wait(pe, reduced, b * H + (h - 1))
                bank = score_banks[:, h % 2, :]
                for qt in range(TT):
                    q = m.qs[r][:, h, qt * P:(qt + 1) * P]
                    if soft:
                        ins = pe.matmul(bank[:, qt * T:(qt + 1) * T], q, m.ks[r][:, h, :], start=True, stop=True)
                    else:
                        first, n = qt * P, (qt + 1) * P
                        pe.matmul(bank[:, first:first + n], q, m.ks[r][:, h, 0:n], start=True, stop=True)
                        ins = pe.matmul(bank[:, first + n - P:first + n], m.ident_b[:, :], m.mask_b[:, :],
                                        start=False, stop=True, skip_group_check=True)
                ins.then_inc(scores_ready, 1)

            def pass2(b, r, p):
                if p == 0:
                    pe.wait_ge(shift_rows, (b + 1) * SEM)
                wait(pe, probs_ready, b * 8 + (p - 1))
                for n in range(2):
                    h = 2 * p + n
                    bank = shifted_banks[:, 2 * (p % 2) + n, :]
                    for kt in range(TT):
                        k = m.ks[r][:, h, kt * P:(kt + 1) * P]
                        if soft:
                            ins = pe.matmul(bank[:, kt * T:(kt + 1) * T], k, m.qs[r][:, h, :], start=True, stop=True)
                        else:
                            first = kt * T
                            pe.matmul(bank[:, first:first + T - kt * P], k, m.qs[r][:, h, kt * P:T],
                                      start=True, stop=True)
                            ins = pe.matmul(bank[:, first:first + P], m.ident_b[:, :], m.maskT_b[:, :],
                                            start=False, stop=True, skip_group_check=True)
                ins.then_inc(shifted_ready, 1)

            def pv(b, r, g):
                pe.wait_ge(probs_ready, b * 8 + (2 * g + 2))
                if g % 2 == 0:
                    wait(pe, ot_ready, b * 2 + g // 2)
                for kt in range(TT):
                    skip = 0 if soft else kt * P
                    for i in range(Q):
                        ins = pe.matmul(out_bank[32 * i:32 * i + 32, (g % 2) * T + skip:(g % 2 + 1) * T],
                                        m.v[r][:, kt, Q * g + i, :],
                                        m.pt[:, g % 2, i, kt * T:(kt + 1) * T - skip],
                                        start=(kt == 0), stop=(kt == TT - 1), skip_group_check=True)
                ins.then_inc(pv_done, 1)

            def slot(t, r):
                for h in range(H):
                    if live(t, 0):
                        if h == 0:
                            transpose_x(t, t)
                        if h == 1:
                            project(t, "q", ["q", "qs"] if soft else ["q", "k"])
                        if h == 3 and soft:
                            project(t, "k", ["k", "ks"])
                        if h == 11:
                            project_v(t)
                    if h == 2 and live(t, 2):
                        transpose_shift(t - 2, t)
                    if h == 6 and live(t, OUT):
                        project_out(t - OUT, t)
                    if live(t, 1):
                        pass1(t - 1, (r - 1) % RING, h)
                    if h % 2 == 1:
                        p, lag = pair_of(h // 2)
                        if live(t, lag):
                            pass2(t - lag, (r - lag) % RING, p)
                        if p % 2 == 0:
                            lag_pv, g = (lag, p // 2 - 1) if p else (lag + 1, 3)
                            if live(t, lag_pv):
                                pv(t - lag_pv, (r - lag_pv) % RING, g)

            def batch(b):
                transpose_x(b, b)
                project(b, "q", ["q", "k"])
                project_v(b)
                for h in range(H):
                    pass1(b, 0, h)
                transpose_shift(b, b)
                for p in range(H // 2):
                    pass2(b, 0, p)
                    if p % 2 == 1:
                        pv(b, 0, p // 2)
                project_out(b, b)

            if general:
                run_batches(pe, batch)
            else:
                run_slots(pe, slot)


def support_phase(nc, ctx, m):
    def sem(name):
        return ctx.enter_context(nc.semaphore(f"support_{name}"))

    flag_step = sem("flag_step")
    counted = sem("counted")

    with nc.Block() as block:
        @block.vector
        def _(dve):
            dve.tensor_reduce(m.flag[:, :], m.worst[:, :, :], AX.XY, ALU.max).then_inc(flag_step, 1)
            dve.wait_ge(flag_step, 1)
            dve.tensor_scalar(m.flag[:, :], m.flag[:, :], 0.0, None, ALU.is_gt).then_inc(flag_step, 1)
            dve.wait_ge(counted, 1)
            dve.tensor_scalar(m.redo[:, :], m.banks[0:1, 0, 0:1], 1.0, None, ALU.min).then_inc(flag_step, 1)
            dve.wait_ge(flag_step, 3)

        @block.tensor
        def _(pe):
            pe.wait_ge(flag_step, 2)
            pe.matmul(m.banks[0:1, 0, 0:1], m.flag[:, :], m.v[0][:, 0, 0, 8:9], start=True, stop=True)\
              .then_inc(counted, 1)


def feed_forward_phase(nc, ctx, m, name, x, out):
    N = 4
    SLOTS = B * TT // N
    NT = N * P

    def sem(what):
        return ctx.enter_context(nc.semaphore(f"{name}_{what}"))

    ln_stats = sem("ln_stats")
    var_ready = sem("var_ready")
    eps_added = sem("eps_added")
    rstd_ready = sem("rstd_ready")
    xhat_ready = sem("xhat_ready")
    turned = sem("turned")
    xT_ready = sem("xT_ready")
    gate_up = sem("gate_up")
    silu_ready = sem("silu_ready")
    hid_ready = sem("hid_ready")
    down_done = sem("down_done")
    x_done = sem("x_done")
    out_stored = sem("out_stored")

    ident = m.cc[:, CC["ident"]:CC["ident"] + P]
    turn_bank = m.banks[:, 0, :]
    gate_banks = m.banks[:, 1:3, :]
    up_banks = m.banks[:, 3:5, :]
    down_banks = m.banks[:, 5:7, :]
    gate_w, up_w, down_w = (m.wf[:, n * HIDDEN:(n + 1) * HIDDEN] for n in range(3))

    def live(t, lag):
        return not isinstance(t, int) or 0 <= t - lag < SLOTS

    def wait(eng, s, value):
        if not isinstance(value, int) or value > 0:
            eng.wait_ge(s, value)

    def run_slots(eng, slot):
        slot(0, 0)
        with eng.Fori(0, (SLOTS - 2) // 2) as n:
            slot(n * 2 + 1, 1)
            slot(n * 2 + 2, 0)
        slot(SLOTS - 1, (SLOTS - 1) % 2)
        slot(SLOTS, SLOTS % 2)

    with nc.Block() as block:

        @block.sync
        def _(sp):
            if out is not None:
                out_d = out.rearrange("b (t p) d -> p (b t) d", p=P)
                with sp.Fori(0, SLOTS) as t:
                    wait_apart(m, sp, x_done, t + 1)
                    sp.dma_start(out_d[:, bass.ds(t * N, N), :], x[:, bass.ds(t * N, N), :]).then_inc(out_stored, SEM)
                sp.wait_ge(out_stored, SLOTS * SEM)

        @block.gpsimd
        def _(pool):
            def rstd(t):
                wait_apart(m, pool, var_ready, t * N + N)
                pool.tensor_scalar(m.ve[:, 0:N], m.mv[:, 0:N, 1], EPS, None, ALU.add).then_inc(eps_added, 1)
                pool.wait_ge(eps_added, t + 1)
                wait(pool, xhat_ready, t * N)
                pool.tensor_tensor(m.rstd[:, 0:N], m.ve[:, 0:N], m.neghalf[:, 0:N], ALU.pow).then_inc(rstd_ready, 1)

            rstd(0)
            with pool.Fori(1, SLOTS) as t:
                rstd(t)

        @block.vector
        def _(dve):
            def layernorm_stats(t):
                wait(dve, xhat_ready, t * N)
                for n in range(N):
                    dve.bn_stats(m.stats[:, n, :], x[:, bass.ds(t * N + n, 1), :].rearrange("p o d -> p (o d)"))\
                       .then_inc(ln_stats, 1)
                wait_apart(m, dve, ln_stats, t * N + N)
                for n in range(N):
                    dve.bn_aggr(m.mv[:, n, :], m.stats[:, n, :]).then_inc(var_ready, 1)

            def layernorm_apply(t):
                dve.wait_ge(rstd_ready, t + 1)
                wait(dve, turned, t)
                for n in range(N):
                    dve.tensor_scalar(m.xhat[:, n, :], x[:, bass.ds(t * N + n, 1), :].rearrange("p o d -> p (o d)"),
                                      m.mv[:, n, 0:1], m.rstd[:, n:n + 1], ALU.subtract, ALU.mult)\
                       .then_inc(xhat_ready, 1)

            def hidden(t, r, c):
                dve.wait_ge(silu_ready, t * NC_H + (c + 1))
                k = (NC_H * r + c) % 2
                dve.tensor_tensor(m.hid[:, r, c, :], m.silu[:, k, :], up_banks[:, k, :], ALU.mult)\
                   .then_inc(hid_ready, 1)

            def residual(t, r):
                dve.wait_ge(down_done, t + 1)
                tiles = x[:, bass.ds(t * N, N), :]
                dve.tensor_tensor(tiles, down_banks[:, r, :].rearrange("p (n d) -> p n d", n=N), tiles, ALU.add)\
                   .then_inc(x_done, 1)

            def slot(t, r):
                if live(t, -1):
                    layernorm_stats(t + 1)
                if live(t, 0):
                    hidden(t, r, 0)
                if live(t, -1):
                    layernorm_apply(t + 1)
                if live(t, 0):
                    hidden(t, r, 1)
                if live(t, 1):
                    residual(t - 1, 1 - r)
                if live(t, 0):
                    hidden(t, r, 2)

            layernorm_stats(0)
            layernorm_apply(0)
            run_slots(dve, slot)

        @block.scalar
        def _(act):
            def take_xT(t, r):
                wait(act, gate_up, (t - 1) * NC_H)
                act.wait_ge(turned, t + 1)
                act.copy(m.xT[:, r, :], turn_bank).then_inc(xT_ready, 1)

            def silu(t, r, c):
                wait(act, hid_ready, t * NC_H + (c - 1))
                act.wait_ge(gate_up, t * NC_H + (c + 1))
                k = (NC_H * r + c) % 2
                act.activation(m.silu[:, k, :], gate_banks[:, k, :], ACT.Silu).then_inc(silu_ready, 1)

            def slot(t, r):
                if live(t, 0):
                    silu(t, r, 0)
                    silu(t, r, 1)
                if live(t, -1):
                    take_xT(t + 1, 1 - r)
                if live(t, 0):
                    silu(t, r, 2)

            take_xT(0, 0)
            run_slots(act, slot)

        @block.tensor
        def _(pe):
            def turn(t):
                pe.wait_ge(xhat_ready, t * N + N)
                wait(pe, xT_ready, t)
                for n in range(N):
                    ins = pe.transpose(turn_bank[:, n * P:(n + 1) * P], m.xhat[:, n, :], ident)
                ins.then_inc(turned, 1)

            def gate_and_up(t, r, c):
                if c == 0:
                    pe.wait_ge(xT_ready, t + 1)
                wait(pe, hid_ready, t * NC_H + (c - 1))
                k = (NC_H * r + c) % 2
                pe.matmul(gate_banks[:, k, :], gate_w[:, c * P:(c + 1) * P], m.xT[:, r, :], start=True, stop=True)
                pe.matmul(up_banks[:, k, :], up_w[:, c * P:(c + 1) * P], m.xT[:, r, :], start=True, stop=True)\
                  .then_inc(gate_up, 1)

            def down(t, r):
                pe.wait_ge(hid_ready, t * NC_H + NC_H)
                for n in range(N):
                    for c in range(NC_H):
                        ins = pe.matmul(down_banks[:, r, n * D:(n + 1) * D], m.hid[:, r, c, n * P:(n + 1) * P],
                                        down_w[:, c * D:(c + 1) * D], start=(c == 0), stop=(c == NC_H - 1))
                ins.then_inc(down_done, 1)

            def slot(t, r):
                if live(t, 0):
                    gate_and_up(t, r, 0)
                if live(t, 1):
                    down(t - 1, 1 - r)
                if live(t, 0):
                    gate_and_up(t, r, 1)
                if live(t, -1):
                    turn(t + 1)
                if live(t, 0):
                    gate_and_up(t, r, 2)

            turn(0)
            run_slots(pe, slot)


def stack_kernel(nc, io):
    with ExitStack() as ctx:
        m = allocate(nc, ctx)
        setup_phase(nc, ctx, m, io)
        attention_phase(nc, ctx, m, io, "a", m.x, m.x)
        feed_forward_phase(nc, ctx, m, "f1", m.x, None)
        attention_phase(nc, ctx, m, io, "b", m.x, m.x2)
        support_phase(nc, ctx, m)
        attention_phase(nc, ctx, m, io, "g", m.x, m.x2)
        feed_forward_phase(nc, ctx, m, "f2", m.x2, io["out"])


def shape_constants():
    f32 = np.float32
    c = np.zeros((P, CC_COLS), f32)
    c[:, CC["ident"]:CC["ident"] + P] = np.eye(P, dtype=f32)
    inv = f32(1.0) / f32(10000.0) ** (np.arange(0, HD, 2, dtype=f32) / f32(HD))
    freqs = np.arange(T, dtype=f32)[:, None] * inv[None, :]
    emb = np.concatenate([freqs, freqs], axis=-1)
    cos, sin = np.cos(emb).astype(f32).T, np.sin(emb).astype(f32).T
    sign = np.where(np.arange(HD) % 2 == 0, f32(-1.0), f32(1.0))[:, None]
    c[:, CC["cos"]:CC["cos"] + T] = np.repeat(cos, H, axis=0)
    c[:, CC["sin"]:CC["sin"] + T] = np.repeat(sin * sign, H, axis=0)
    q, k = np.arange(P)[:, None], np.arange(P)[None, :]
    c[:, CC["mask"]:CC["mask"] + P] = np.where(k > q, f32(NEG), f32(0.0))
    c[:, CC["maskT"]:CC["maskT"] + P] = np.where(q > k, f32(NEG), f32(0.0))
    c[:, CC["invk"]:CC["invk"] + 256] = np.tile(f32(1.0) / np.arange(1, 9, dtype=f32), 32)
    c[:, CC["seg"]:CC["seg"] + 256] = np.tile(np.arange(8) > 0, 32)
    return c


def kernel(**inputs):
    import concourse.bacc as _bacc
    from concourse.bass_utils import run_bass_kernel_spmd as _run

    a = {n: np.asarray(v) for n, v in inputs.items()}
    dm = np.arange(D).reshape(H, HD).T.reshape(-1)
    dms = np.arange(D).reshape(H, HD)[:, np.arange(HD) ^ 1].T.reshape(-1)
    idg = np.arange(D).reshape(Q, Q, HD).transpose(1, 2, 0).reshape(-1)

    def spread(v):
        return np.broadcast_to(v, (P, D))

    wa = np.concatenate([
        a["L0_attn_a_Wq"].T[:, dm], a["L0_attn_a_Wq"].T[:, dms], a["L0_attn_a_Wk"].T[:, dm],
        a["L0_attn_a_Wk"].T[:, dms], a["L0_attn_a_Wv"].T, a["L0_attn_a_Wo"].T[idg],
        a["L0_attn_a_bq"][dm, None], a["L0_attn_a_bq"][dms, None], a["L0_attn_a_bk"][dm, None],
        a["L0_attn_a_bk"][dms, None], spread(a["L0_attn_a_bv"]), spread(a["L0_attn_a_bo"])], axis=1)
    wat, bat = a["L0_attn_b_w_attn"], a["L0_attn_b_b_attn"]
    wb = np.concatenate([
        wat[:, 0:D][:, dm], wat[:, D:2 * D][:, dm], wat[:, 2 * D:], a["L0_attn_b_w_proj"][idg],
        bat[0:D][dm, None], bat[D:2 * D][dm, None], spread(bat[2 * D:]), spread(a["L0_attn_b_b_proj"])], axis=1)
    wf = np.concatenate([
        a["L0_ffn_w_gate"].T, a["L0_ffn_w_up"].T,
        a["L0_ffn_w_down"].T.reshape(NC_H, P, D).transpose(1, 0, 2).reshape(P, HIDDEN)], axis=1)
    arrays = {"x": a["L0_attn_a_x"], "wa": wa, "wb": wb, "wf": wf, "consts": shape_constants()}
    arrays = {n: np.ascontiguousarray(v) for n, v in arrays.items()}

    nc = _bacc.Bacc("TRN2", target_bir_lowering=False, num_devices=1)
    io = {n: nc.dram_tensor(n + "_in", v.shape, mybir.dt.from_np(v.dtype), kind="ExternalInput").ap()
          for n, v in arrays.items()}
    io["out"] = nc.dram_tensor("out_0", (B, T, D), F32, kind="ExternalOutput").ap()
    stack_kernel(nc, io)
    r = _run(nc, [{n + "_in": v for n, v in arrays.items()}], core_ids=[0])
    return r.results[0]["out_0"]
```

```python
from contextlib import ExitStack

import concourse.bass as bass
from concourse import mybir
import numpy as np

F32 = mybir.dt.float32
BF16 = mybir.dt.bfloat16
I32 = mybir.dt.int32
ALU = mybir.AluOpType
ACT = mybir.ActivationFunctionType
AX = mybir.AxisListType

B, T, D, H = 16, 256, 128, 16
HD = D // H
P = 128
TT = T // P
HIDDEN = 384
NC_H = HIDDEN // P
EPS = 1e-5
SCALE = float(np.float32(1.0) / np.sqrt(np.float32(HD)))
STACKS = 4
PARTS = 3
STACK = PARTS * PARTS * HD
NEG = -1.0e30
BISECTIONS = 28
Q = 4
SEM = 16

WA = dict(q=0, qs=128, k=256, ks=384, v=512, o=640, bq=768, bqs=769, bk=770, bks=771, bv=772, bo=900)
WA_COLS = 1028
WB = dict(q=0, k=128, v=256, o=384, bq=512, bk=513, bv=514, bo=642)
WB_COLS = 770
CC = dict(ident=0, cos=128, sin=384, mask=640, maskT=768, invk=896, seg=1152)
CC_COLS = 1408


class Places:
    pass


def allocate(nc, ctx):
    m = Places()

    def sb(name, shape, dt=F32):
        return ctx.enter_context(nc.sbuf_tensor(name, shape, dt))

    m.x = sb("x", [P, (B + 1) * TT, D])
    m.x2 = sb("x2", [P, B * TT, D])
    m.wa = sb("wa", [P, WA_COLS])
    m.wb = sb("wb", [P, WB_COLS])
    m.wf_int = sb("wf_int", [P, 3 * HIDDEN], I32)
    m.wf = sb("wf", [P, 3 * HIDDEN])
    m.cc = sb("cc", [P, CC_COLS])
    m.ident_b = sb("ident_b", [P, P], BF16)
    m.mask_b = sb("mask_b", [P, P], BF16)
    m.maskT_b = sb("maskT_b", [P, P], BF16)
    m.neghalf = sb("neghalf", [P, 4])
    m.zero_rows = sb("zero_rows", [PARTS * H, T], BF16)
    m.one_rows = sb("one_rows", [PARTS * H, T], BF16)
    m.qs = [sb(f"q_stack{r}", [P, H, T], BF16) for r in range(STACKS)]
    m.ks = [sb(f"k_stack{r}", [P, H, T], BF16) for r in range(STACKS)]
    m.v = [sb(f"v_ext{r}", [P, TT, H, 32]) for r in range(STACKS)]
    m.pt = sb("probs_t", [P, 2, Q, 2 * T])
    m.stats = sb("bn_out", [P, 4, 6])
    m.mv = sb("mean_var", [P, 4, 2])
    m.ve = sb("var_eps", [P, 4])
    m.rstd = sb("rstd", [P, 4])
    m.xhat = sb("xhat", [P, 4, D])
    m.xT = sb("xT", [P, 2, 512])
    m.tc = sb("rope_cos_terms", [P, 2, T])
    m.ts = sb("rope_sin_terms", [P, 2, T])
    m.qk = sb("qk", [P, 2, T])
    m.parts = sb("qk_parts", [P, PARTS, 2, T], BF16)
    m.nm = sb("neg_shift", [P, STACKS, H, TT])
    m.nm_rest = sb("neg_shift_rest", [P, H, TT])
    m.nm_parts = sb("neg_shift_parts", [P, TT, PARTS, H], BF16)
    m.nmT = sb("neg_shift_rows", [PARTS * H, T], BF16)
    m.ot = sb("out_t", [P, Q, T])
    m.oc = sb("out_compact", [P, T])
    m.den = sb("denominators", [P, T])
    m.rden = sb("rdenominators", [P, T])
    m.ocn = sb("out_normal", [P, T])
    m.xb = sb("x_plus_bias", [P, TT, D])
    m.z8 = sb("top8", [P, 2, H, TT, 8])
    m.cs = sb("top8_sums", [P, H, TT, 8])
    m.excess = sb("excess", [P, H, TT])
    m.worst = sb("worst", [P, H, TT])
    m.flag = sb("flag", [P, 1])
    m.redo = sb("redo", [1, 1], I32)
    m.z_max, m.low, m.width, m.mid, m.z_sum = (sb(n, [P, TT]) for n in ("z_max", "low", "width", "mid", "z_sum"))
    m.z_rows = sb("z_rows", [P, TT, T])
    m.z_work = sb("z_work", [P, TT, T])
    m.silu = sb("silu", [P, 2, 512])
    m.hid = sb("hidden", [P, 2, NC_H, 512])
    m.banks = ctx.enter_context(nc.psum_tensor("banks", [P, 8, 512], F32))
    m.passed = {e.engine: ctx.enter_context(nc.semaphore(f"passed_{n}"))
                for n, e in (("sp", nc.sync), ("pool", nc.gpsimd), ("dve", nc.vector), ("pe", nc.tensor))}
    return m


def wait_apart(m, eng, s, value):
    if not isinstance(value, int):
        eng.wait_ge(s, value)
        eng.sem_inc(m.passed[eng.engine], 1)
    elif value > 0:
        eng.wait_ge(s, value)


def setup_phase(nc, ctx, m, io):
    def sem(name):
        return ctx.enter_context(nc.semaphore(name))

    loaded_a = sem("loaded_a")
    m.rest_loaded = sem("rest_loaded")
    m.dequantised = sem("dequantised")
    zeroed = sem("zeroed")
    ones_set = sem("ones_set")
    ones_rows = sem("ones_rows")
    x_loaded = sem("x_loaded")
    consts = sem("consts_ready")
    x_d = io["x"].rearrange("b (t p) d -> p (b t) d", p=P)

    with nc.Block() as block:
        @block.sync
        def _(sp):
            sp.dma_start(m.x[:, 0:TT, :], x_d[:, 0:TT, :]).then_inc(x_loaded, SEM)
            sp.dma_start(m.cc[:, :], io["consts"]).then_inc(loaded_a, SEM)
            sp.dma_start(m.wa[:, :], io["wa"]).then_inc(loaded_a, SEM)
            sp.dma_start(m.x[:, TT:B * TT, :], x_d[:, TT:B * TT, :]).then_inc(m.rest_loaded, SEM)
            sp.dma_start(m.wf_int[:, :], io["wf"]).then_inc(m.rest_loaded, SEM)
            sp.dma_start(m.wb[:, :], io["wb"]).then_inc(m.rest_loaded, SEM)
            sp.wait_ge(ones_set, 1)
            sp.wait_ge(zeroed, 2 * STACKS)
            for r in range(STACKS):
                sp.dma_start(m.ks[r][STACK:STACK + PARTS, :, :], m.one_rows[:, :]).then_inc(ones_rows, SEM)
            sp.wait_ge(ones_rows, STACKS * SEM)
            sp.wait_ge(x_loaded, SEM)

        @block.gpsimd
        def _(pool):
            pool.memset(m.one_rows[:, :], 1.0).then_inc(ones_set, 1)
            pool.memset(m.neghalf[:, :], -0.5).then_inc(consts, 1)
            for r in range(STACKS):
                pool.memset(m.qs[r][:, :, :].bitcast(F32), 0.0).then_inc(zeroed, 1)

        @block.vector
        def _(dve):
            for r in range(STACKS):
                dve.memset(m.ks[r][:, :, :].bitcast(F32), 0.0).then_inc(zeroed, 1)
            dve.memset(m.x[:, B * TT:, :], 0.0).then_inc(consts, 1)
            dve.memset(m.worst[:, :, :], -1.0).then_inc(consts, 1)
            dve.memset(m.zero_rows[:, :], 0.0).then_inc(consts, 1)
            for r in range(STACKS):
                dve.memset(m.v[r][:, :, :, 8:32], 1.0).then_inc(consts, 1)
            dve.wait_ge(loaded_a, 2 * SEM)
            dve.tensor_copy(m.ident_b[:, :], m.cc[:, CC["ident"]:CC["ident"] + P]).then_inc(consts, 1)
            dve.tensor_copy(m.mask_b[:, :], m.cc[:, CC["mask"]:CC["mask"] + P]).then_inc(consts, 1)
            dve.tensor_copy(m.maskT_b[:, :], m.cc[:, CC["maskT"]:CC["maskT"] + P]).then_inc(consts, 1)


def attention_phase(nc, ctx, m, io, kind, x_in, x_out):
    soft = kind == "a"
    general = kind == "g"
    w, at = (m.wa, WA) if soft else (m.wb, WB)

    def sem(name):
        return ctx.enter_context(nc.semaphore(f"{kind}_{name}"))

    ln_stats = sem("ln_stats")
    var_ready = sem("var_ready")
    eps_added = sem("eps_added")
    rstd_ready = sem("rstd_ready")
    xhat_ready = sem("xhat_ready")
    dense_full = sem("dense_full")
    dense_free = sem("dense_free")
    q_step = sem("q_step")
    k_step = sem("k_step")
    q_split = sem("q_split")
    k_split = sem("k_split")
    q_stored = sem("q_stored")
    k_stored = sem("k_stored")
    stack_loaded = sem("stack_loaded")
    scores_ready = sem("scores_ready")
    reduced = sem("reduced")
    shift_step = sem("shift_step")
    shift_split = sem("shift_split")
    shift_rows = sem("shift_rows")
    shifted_ready = sem("shifted_ready")
    probs_ready = sem("probs_ready")
    pv_done = sem("pv_done")
    ot_ready = sem("ot_ready")
    ot_stored = sem("ot_stored")
    oc_loaded = sem("oc_loaded")
    rden_ready = sem("rden_ready")
    ocn_ready = sem("ocn_ready")
    xb_ready = sem("xb_ready")
    tau_step = sem("tau_step")
    excess_ready = sem("excess_ready")
    worst_noted = sem("worst_noted")

    q_image = nc.dram_tensor(f"{kind}_q_image", [5, P, T], BF16, kind="Internal").ap()
    k_image = nc.dram_tensor(f"{kind}_k_image", [PARTS, P, T], BF16, kind="Internal").ap()
    o_image = nc.dram_tensor(f"{kind}_o_image", [Q, 32, Q, T], F32, kind="Internal").ap()
    q_rows = q_image.rearrange("s (d h) t -> (s d) h t", h=H)
    k_rows = k_image.rearrange("s (d h) t -> (s d) h t", h=H)
    o_rows = o_image.rearrange("i d g t -> i (d g) t")

    ident = m.cc[:, CC["ident"]:CC["ident"] + P]
    score_banks = m.banks[:, 0:2, :]
    shifted_banks = m.banks[:, 2:6, :]
    out_bank = m.banks[:, 6, :]
    dense = m.banks[:, 7, :]
    dense_b = m.banks[:, 7:8, :].bitcast(BF16)

    if general:
        USES = [("xT", 0), ("q", 0), ("v", 0), ("shift", 0), ("proj", 0)]
        FIRST = 1
        RING = 1
    else:
        USES = [("xT", 0), ("q", 0)] + ([("k", 0)] if soft else []) + [("shift", 2), ("proj", 4), ("v", 0)]
        FIRST = 4
        RING = STACKS
    AT = dict(xT=0, q=2, k=4, shift=7, proj=11, v=13, apply=10, normalise=7, invert=(5, 6))
    if not soft:
        AT = dict(xT=0, q=1, shift=8, proj=11, v=13, apply=10, support=9)
    LATE1, LATE2 = 3, 5
    OUT = dict(USES)["proj"]
    SLOTS = B + OUT

    def live(t, lag):
        return not isinstance(t, int) or 0 <= t - lag < B

    def uses_before(t, use):
        inside = [n for n, _ in USES].index(use)
        if isinstance(t, int):
            return (sum(live(s, lag) for s in range(t) for _, lag in USES)
                    + sum(live(t, lag) for _, lag in USES[:inside]))
        first = sum(live(s, lag) for s in range(FIRST) for _, lag in USES)
        return (t - FIRST) * len(USES) + (first + inside)

    def sums_done(t):
        return uses_before(t, "proj") + 1 if live(t, OUT) else 0

    def wait(eng, s, value):
        if not isinstance(value, int) or value > 0:
            eng.wait_ge(s, value)

    def run_slots(eng, slot):
        turns = (B - FIRST) // RING
        for t in range(FIRST):
            slot(t, t % RING)
        with eng.Fori(0, turns) as n:
            for k in range(RING):
                slot(n * RING + (FIRST + k), (FIRST + k) % RING)
        for t in range(FIRST + turns * RING, SLOTS):
            slot(t, t % RING)

    def run_batches(eng, batch):
        redo = eng.value_load(m.redo[0:1, 0:1], min_val=0, max_val=1)
        with eng.If(redo > 0):
            run_slots(eng, lambda b, r: batch(b))

    def head_of(s):
        return (s - LATE1) % H, (1 if s >= LATE1 else 2)

    def pair_of(j):
        return (j - LATE2) % 8, (2 if j >= LATE2 else 3)

    with nc.Block() as block:

        @block.sync
        def _(sp):
            def store_q(b):
                wait_apart(m, sp, q_split, b + 1)
                wait(sp, stack_loaded, b * (7 * SEM))
                sp.dma_start(q_image[0:3].rearrange("s p t -> p s t"), m.parts[:, :, 0, :]).then_inc(q_stored, SEM)
                sp.dma_start(q_image[3:5].rearrange("s p t -> p s t"), m.parts[:, 0:2, 0, :]).then_inc(q_stored, SEM)

            def store_k(b):
                wait_apart(m, sp, k_split, b + 1)
                sp.dma_start(k_image.rearrange("s p t -> p s t"), m.parts[:, :, 1, :]).then_inc(k_stored, SEM)

            def load_q(b, r):
                wait_apart(m, sp, q_stored, (b + 1) * (2 * SEM))
                wait(sp, shifted_ready, (b - (RING - 1)) * 8)
                sp.dma_start(m.qs[r][STACK:STACK + PARTS, :, :], m.zero_rows[:, :]).then_inc(stack_loaded, SEM)
                for rep in range(PARTS):
                    rows = slice(rep * PARTS * HD, (rep + 1) * PARTS * HD)
                    sp.dma_start(m.qs[r][rows, :, :], q_rows[rep * HD:(rep + PARTS) * HD]).then_inc(stack_loaded, SEM)

            def load_k(b, r):
                wait_apart(m, sp, k_stored, (b + 1) * SEM)
                for rep in range(PARTS):
                    rows = slice(rep * PARTS * HD, (rep + 1) * PARTS * HD)
                    sp.dma_start(m.ks[r][rows, :, :], k_rows[0:PARTS * HD]).then_inc(stack_loaded, SEM)

            def load_shift(b, t, r):
                wait_apart(m, sp, dense_free, uses_before(t, "shift") + 1)
                sp.dma_start(m.qs[r][STACK:STACK + PARTS, :, :], m.nmT[:, :]).then_inc(shift_rows, SEM)

            def store_out(b):
                wait_apart(m, sp, ot_ready, b * 2 + 2)
                wait(sp, oc_loaded, b * ((2 if soft else 1) * SEM))
                sp.dma_start(o_image.rearrange("i d g t -> (i d) g t"), m.ot[:, :, :]).then_inc(ot_stored, SEM)

            def load_out(b, t):
                wait_apart(m, sp, ot_stored, (b + 1) * SEM)
                if soft:
                    wait(sp, ocn_ready, b)
                else:
                    wait(sp, dense_free, sums_done(t - 1 if general else t))
                sp.dma_start(m.oc[:, :], o_rows[:, 0:HD * Q, :]).then_inc(oc_loaded, SEM)
                if soft:
                    sp.dma_start(m.den[:, :], o_rows[:, HD * Q:2 * HD * Q, :]).then_inc(oc_loaded, SEM)

            def slot(t, r):
                if live(t, 0):
                    store_q(t)
                if live(t, 2):
                    load_shift(t - 2, t, (r - 2) % RING)
                if live(t, 0):
                    store_k(t)
                    load_q(t, r)
                    load_k(t, r)
                if live(t, 3):
                    store_out(t - 3)
                    load_out(t - 3, t)

            def batch(b):
                store_q(b)
                store_k(b)
                load_q(b, 0)
                load_k(b, 0)
                load_shift(b, b, 0)
                store_out(b)
                load_out(b, b)

            if general:
                run_batches(sp, batch)
            else:
                run_slots(sp, slot)

        @block.gpsimd
        def _(pool):
            def rstd(b):
                wait_apart(m, pool, var_ready, b * 2 + 2)
                pool.tensor_scalar(m.ve[:, 0:TT], m.mv[:, 0:TT, 1], EPS, None, ALU.add).then_inc(eps_added, 1)
                pool.wait_ge(eps_added, b + 1)
                wait(pool, xhat_ready, b * 2)
                pool.tensor_tensor(m.rstd[:, 0:TT], m.ve[:, 0:TT], m.neghalf[:, 0:TT], ALU.pow).then_inc(rstd_ready, 1)

            def split_shift(b, r):
                if soft or general:
                    pool.wait_ge(reduced, (b + 1) * H)
                else:
                    pool.wait_ge(tau_step, b * 3 + 3)
                wait_apart(m, pool, shift_rows, b * SEM)
                nm = m.nm[:, r, :, :]
                out = [m.nm_parts[:, :, n, :].rearrange("p q h -> p h q") for n in range(PARTS)]
                pool.tensor_copy(out[0], nm).then_inc(shift_step, 1)
                pool.wait_ge(shift_step, b * 3 + 1)
                pool.tensor_tensor(m.nm_rest[:, :, :], nm, out[0], ALU.subtract).then_inc(shift_step, 1)
                wait_apart(m, pool, shift_step, b * 3 + 2)
                pool.tensor_copy(out[1], m.nm_rest[:, :, :]).then_inc(shift_step, 1)
                pool.wait_ge(shift_step, b * 3 + 3)
                pool.tensor_tensor(out[2], m.nm_rest[:, :, :], out[1], ALU.subtract).then_inc(shift_split, 1)

            def split(b, t, n):
                step, done = ((q_step, q_split), (k_step, k_split))[n]
                pool.wait_ge(dense_free, uses_before(t, "k" if soft and n else "q") + 1)
                if soft:
                    pool.tensor_tensor(m.qk[:, n, :], m.tc[:, n, :], m.ts[:, n, :], ALU.add).then_inc(step, 1)
                    pool.wait_ge(step, b * 4 + 1)
                base = b * 4 + 1 if soft else b * 3
                wait_apart(m, pool, k_stored if n else q_stored, b * (SEM if n else 2 * SEM))
                pool.tensor_copy(m.parts[:, 0, n, :], m.qk[:, n, :]).then_inc(step, 1)
                pool.wait_ge(step, base + 1)
                pool.tensor_tensor(m.qk[:, n, :], m.qk[:, n, :], m.parts[:, 0, n, :], ALU.subtract).then_inc(step, 1)
                wait_apart(m, pool, step, base + 2)
                pool.tensor_copy(m.parts[:, 1, n, :], m.qk[:, n, :]).then_inc(step, 1)
                pool.wait_ge(step, base + 3)
                pool.tensor_tensor(m.parts[:, 2, n, :], m.qk[:, n, :], m.parts[:, 1, n, :], ALU.subtract).then_inc(done, 1)

            def add_bias(b, t):
                wait(pool, dense_free, sums_done(t - 1))
                for tt in range(TT):
                    pool.tensor_tensor(m.xb[:, tt, :], x_in[:, bass.ds(b * TT + tt, 1), :].rearrange("p o d -> p (o d)"), w[:, at["bo"]:at["bo"] + D],
                                       ALU.add).then_inc(xb_ready, 1)

            def slot(t, r):
                if live(t, OUT):
                    add_bias(t - OUT, t)
                if live(t, -1):
                    rstd(t + 1)
                if live(t, 0) and not soft:
                    split(t, t, 0)
                if live(t, 2):
                    split_shift(t - 2, (r - 2) % RING)
                if live(t, 0) and soft:
                    split(t, t, 0)
                if live(t, 0):
                    split(t, t, 1)

            def batch(b):
                rstd(b)
                split(b, b, 0)
                split(b, b, 1)
                split_shift(b, 0)
                add_bias(b, b)

            if general:
                run_batches(pool, batch)
            else:
                rstd(0)
                run_slots(pool, slot)

        @block.vector
        def _(dve):
            def layernorm_stats(b):
                wait(dve, xhat_ready, b * 2)
                for tt in range(TT):
                    dve.bn_stats(m.stats[:, tt, :], x_in[:, bass.ds(b * TT + tt, 1), :].rearrange("p o d -> p (o d)")).then_inc(ln_stats, 1)
                wait_apart(m, dve, ln_stats, b * 2 + 2)
                for tt in range(TT):
                    dve.bn_aggr(m.mv[:, tt, :], m.stats[:, tt, :]).then_inc(var_ready, 1)

            def layernorm_apply(b, t):
                dve.wait_ge(rstd_ready, b + 1)
                if isinstance(b, int) and b == 0:
                    pass
                else:
                    dve.wait_ge(dense_full, uses_before(t, "xT") + 1)
                for tt in range(TT):
                    dve.tensor_scalar(m.xhat[:, tt, :], x_in[:, bass.ds(b * TT + tt, 1), :].rearrange("p o d -> p (o d)"), m.mv[:, tt, 0:1],
                                      m.rstd[:, tt:tt + 1], ALU.subtract, ALU.mult).then_inc(xhat_ready, 1)

            def rope(b, t, n, use):
                wait(dve, (q_split, k_split)[n], b)
                dve.wait_ge(dense_full, uses_before(t, use) + 1)
                bias, bias_s = at["b" + use], at["b" + use + "s"]
                dve.scalar_tensor_tensor(m.tc[:, n, :], dense[:, 0:T], w[:, bias:bias + 1],
                                         m.cc[:, CC["cos"]:CC["cos"] + T], ALU.add, ALU.mult)
                dve.scalar_tensor_tensor(m.ts[:, n, :], dense[:, T:2 * T], w[:, bias_s:bias_s + 1],
                                         m.cc[:, CC["sin"]:CC["sin"] + T], ALU.add, ALU.mult).then_inc(dense_free, 1)

            def take_qk(b, t):
                wait(dve, k_split, b)
                dve.wait_ge(dense_full, uses_before(t, "q") + 1)
                dve.tensor_scalar(m.qk[:, 0, :], dense[:, 0:T], w[:, at["bq"]:at["bq"] + 1], SCALE, ALU.add, ALU.mult)
                dve.tensor_scalar(m.qk[:, 1, :], dense[:, T:2 * T], w[:, at["bk"]:at["bk"] + 1], None,
                                  ALU.add).then_inc(dense_free, 1)

            def take_v(b, t, r):
                wait(dve, pv_done, (b - (RING - 1)) * 4)
                dve.wait_ge(dense_full, uses_before(t, "v") + 1)
                bv = w[:, at["bv"]:at["bv"] + D].rearrange("p (h d) -> p h d", d=HD)
                for tt in range(TT):
                    ins = dve.tensor_tensor(m.v[r][:, tt, :, 0:HD],
                                            dense[:, tt * D:(tt + 1) * D].rearrange("p (h d) -> p h d", d=HD),
                                            bv, ALU.add)
                    if tt == TT - 1:
                        ins.then_inc(dense_free, 1)

            def reduce_head(b, r, h):
                wait_apart(m, dve, scores_ready, b * H + (h + 1))
                bank = score_banks[:, h % 2, :]
                if soft:
                    dve.tensor_reduce(m.nm[:, r, h, :], bank.rearrange("p (q k) -> p q k", q=TT), AX.X, ALU.max,
                                      negate=True).then_inc(reduced, 1)
                else:
                    dve.max(m.z8[:, r % 2, h, 0, :], bank[:, 0:P])
                    dve.max(m.z8[:, r % 2, h, 1, :], bank[:, P:P + T]).then_inc(reduced, 1)

            def tau(b, r):
                z = m.z8[:, r % 2, :, :, :].rearrange("p h q k -> p (h q k)")
                cs = m.cs[:, :, :, :].rearrange("p h q k -> p (h q k)")
                c = m.cs[:, :, :, :].rearrange("p h q k -> p (h q) k")
                dve.wait_ge(reduced, (b + 1) * H)
                dve.tensor_tensor_scan(cs, m.cc[:, CC["seg"]:CC["seg"] + 256], z, 0.0, ALU.mult,
                                       ALU.add).then_inc(tau_step, 1)
                dve.wait_ge(tau_step, b * 3 + 1)
                dve.scalar_tensor_tensor(cs, cs, -1.0, m.cc[:, CC["invk"]:CC["invk"] + 256], ALU.add,
                                         ALU.mult).then_inc(tau_step, 1)
                dve.wait_ge(tau_step, b * 3 + 2)
                dve.tensor_reduce(m.nm[:, r, :, :].rearrange("p h q -> p (h q)"), c, AX.X, ALU.max,
                                  negate=True).then_inc(tau_step, 1)

            def support_excess(b, r):
                wait(dve, worst_noted, b)
                wait_apart(m, dve, tau_step, b * 3 + 3)
                dve.tensor_tensor(m.excess[:, :, :], m.z8[:, r % 2, :, :, 7], m.nm[:, r, :, :], ALU.add)\
                   .then_inc(excess_ready, 1)

            def note_worst(b):
                dve.wait_ge(excess_ready, b + 1)
                dve.tensor_tensor(m.worst[:, :, :], m.worst[:, :, :], m.excess[:, :, :], ALU.max).then_inc(worst_noted, 1)

            def bisect_head(b, h):
                wait_apart(m, dve, scores_ready, b * H + (h + 1))
                bank = score_banks[:, h % 2, :]
                rows = (bank[:, 0:P], bank[:, P:P + T])
                z = (m.z_rows[:, 0, 0:P], m.z_rows[:, 1, :])
                for q in range(TT):
                    dve.tensor_reduce(m.z_max[:, q:q + 1], rows[q], AX.X, ALU.max)
                dve.memset(m.z_rows[:, 0, P:T], NEG)
                dve.memset(m.low[:, :], -1.0)
                dve.memset(m.width[:, :], 0.5)
                dve.drain()
                for q in range(TT):
                    ins = dve.tensor_scalar(z[q], rows[q], m.z_max[:, q:q + 1], None, ALU.subtract)
                dve.drain()
                with dve.Fori(0, BISECTIONS):
                    dve.tensor_tensor(m.mid[:, :], m.low[:, :], m.width[:, :], ALU.add)
                    dve.drain()
                    for q in range(TT):
                        dve.tensor_scalar(m.z_work[:, q, :], m.z_rows[:, q, :], m.mid[:, q:q + 1], 0.0,
                                          ALU.subtract, ALU.max)
                    dve.drain()
                    dve.tensor_reduce(m.z_sum[:, :], m.z_work[:, :, :], AX.X, ALU.add)
                    dve.drain()
                    dve.tensor_scalar(m.z_sum[:, :], m.z_sum[:, :], 1.0, None, ALU.is_ge)
                    dve.drain()
                    dve.tensor_tensor(m.z_sum[:, :], m.z_sum[:, :], m.width[:, :], ALU.mult)
                    dve.drain()
                    dve.tensor_tensor(m.low[:, :], m.low[:, :], m.z_sum[:, :], ALU.add)
                    dve.tensor_scalar(m.width[:, :], m.width[:, :], 0.5, None, ALU.mult)
                    dve.drain()
                for q in range(TT):
                    dve.tensor_scalar(m.z_work[:, q, :], m.z_rows[:, q, :], m.low[:, q:q + 1], None, ALU.is_gt)
                dve.drain()
                dve.tensor_reduce(m.mid[:, :], m.z_work[:, :, :], AX.X, ALU.add)
                dve.drain()
                dve.tensor_tensor(m.z_work[:, :, :], m.z_work[:, :, :], m.z_rows[:, :, :], ALU.mult)
                dve.drain()
                dve.tensor_reduce(m.z_sum[:, :], m.z_work[:, :, :], AX.X, ALU.add)
                dve.reciprocal(m.mid[:, :], m.mid[:, :])
                dve.drain()
                dve.scalar_tensor_tensor(m.z_sum[:, :], m.z_sum[:, :], -1.0, m.mid[:, :], ALU.add, ALU.mult)
                dve.drain()
                dve.tensor_tensor(m.z_sum[:, :], m.z_sum[:, :], m.z_max[:, :], ALU.add)
                dve.drain()
                if h == 0:
                    wait(dve, shift_split, b)
                dve.tensor_scalar(m.nm[:, 0, h, :], m.z_sum[:, :], -1.0, None, ALU.mult).then_inc(reduced, 1)

            def invert(b, half):
                wait(dve, ocn_ready, b)
                dve.wait_ge(oc_loaded, (b + 1) * (2 * SEM))
                tokens = slice(half * P, (half + 1) * P)
                dve.reciprocal(m.rden[:, tokens], m.den[:, tokens]).then_inc(rden_ready, 1)

            def normalise(b, t):
                wait(dve, dense_full, sums_done(t - 1))
                dve.wait_ge(rden_ready, b * 2 + 2)
                dve.tensor_tensor(m.ocn[:, :], m.oc[:, :], m.rden[:, :], ALU.mult).then_inc(ocn_ready, 1)

            def residual(b, t):
                dve.wait_ge(dense_full, uses_before(t, "proj") + 1)
                dve.wait_ge(xb_ready, b * 2 + 2)
                dve.tensor_tensor(x_out[:, bass.ds(b * TT, TT), :], dense[:, 0:TT * D].rearrange("p (q d) -> p q d", q=TT),
                                  m.xb[:, :, :], ALU.add).then_inc(dense_free, 1)

            def slot(t, r):
                for h in range(H):
                    if h == 0 and live(t, -1):
                        layernorm_stats(t + 1)
                    head, lag = head_of(h)
                    if live(t, lag):
                        reduce_head(t - lag, (r - lag) % RING, head)
                        if head == H - 1 and not soft:
                            tau(t - lag, (r - lag) % RING)
                    if live(t, 0):
                        if h == AT["q"]:
                            rope(t, t, 0, "q") if soft else take_qk(t, t)
                        if soft and h == AT["k"]:
                            rope(t, t, 1, "k")
                        if h == AT["v"]:
                            take_v(t, t, r)
                    if not soft and h == AT["support"] and live(t, 2):
                        support_excess(t - 2, (r - 2) % RING)
                    if not soft and h == AT["support"] + 1 and live(t, 2):
                        note_worst(t - 2)
                    if h == AT["apply"] and live(t, -1):
                        layernorm_apply(t + 1, t)
                    if soft and h in AT["invert"] and live(t, OUT):
                        invert(t - OUT, AT["invert"].index(h))
                    if soft and h == AT["normalise"] and live(t, OUT):
                        normalise(t - OUT, t)
                    if h == AT["proj"] and live(t, OUT):
                        residual(t - OUT, t)

            def batch(b):
                layernorm_stats(b)
                layernorm_apply(b, b - 1)
                take_qk(b, b)
                take_v(b, b, 0)
                for h in range(H):
                    bisect_head(b, h)
                residual(b, b)

            if general:
                run_batches(dve, batch)
            else:
                layernorm_stats(0)
                layernorm_apply(0, 0)
                if soft:
                    dve.wait_ge(m.rest_loaded, 3 * SEM)
                run_slots(dve, slot)
                if soft:
                    dve.tensor_scalar(m.wf[:, :], m.wf_int[:, :], float(np.float32(1.0 / 127.0)), None,
                                      ALU.mult).then_inc(m.dequantised, 1)

        @block.scalar
        def _(act):
            def take_xT(t):
                act.wait_ge(dense_full, uses_before(t, "xT") + 1)
                act.copy(m.xT[:, 0, 0:T], dense[:, 0:T]).then_inc(dense_free, 1)

            def take_shift(b, t):
                wait(act, shift_rows, b * SEM)
                act.wait_ge(dense_full, uses_before(t, "shift") + 1)
                act.copy(m.nmT[:, :], dense_b[0:PARTS * H, 0, 0:T]).then_inc(dense_free, 1)

            def probs(b, p):
                wait(act, pv_done, b * 4 + (p // 2 - 1))
                act.wait_ge(shifted_ready, b * 8 + (p + 1))
                n = 2 * T if soft else T + P
                act.activation(m.pt[:, (p // 2) % 2, 2 * (p % 2):2 * (p % 2) + 2, 0:n],
                               shifted_banks[:, 2 * (p % 2):2 * (p % 2) + 2, 0:n],
                               ACT.Exp if soft else ACT.Relu, scale=SCALE if soft else 1.0).then_inc(probs_ready, 1)

            def take_out(b, half):
                act.wait_ge(pv_done, b * 4 + (2 * half + 2))
                if half == 0:
                    wait(act, ot_stored, b * SEM)
                act.copy(m.ot[:, 2 * half:2 * half + 2, :],
                         out_bank.rearrange("p (g t) -> p g t", g=2)).then_inc(ot_ready, 1)

            def slot(t, r):
                if live(t, 0):
                    take_xT(t)
                for j in range(8):
                    p, lag = pair_of(j)
                    if j == AT["shift"] // 2 and live(t, 2):
                        take_shift(t - 2, t)
                    if live(t, lag):
                        probs(t - lag, p)
                    if p == 4 and live(t, lag):
                        take_out(t - lag, 0)
                    if p == 0 and live(t, lag + 1):
                        take_out(t - lag - 1, 1)

            def batch(b):
                take_xT(b)
                take_shift(b, b)
                for p in range(H // 2):
                    probs(b, p)
                    if p % 4 == 3:
                        take_out(b, p // 4)

            if general:
                run_batches(act, batch)
            else:
                run_slots(act, slot)

        @block.tensor
        def _(pe):
            def transpose_x(b, t):
                pe.wait_ge(xhat_ready, b * 2 + 2)
                wait(pe, dense_free, uses_before(t, "xT"))
                for tt in range(TT):
                    ins = pe.transpose(dense[:, tt * P:(tt + 1) * P], m.xhat[:, tt, :], ident)
                ins.then_inc(dense_full, 1)

            def project(t, use, names):
                pe.wait_ge(dense_free, uses_before(t, use))
                for n, name in enumerate(names):
                    ins = pe.matmul(dense[:, n * T:(n + 1) * T], w[:, at[name]:at[name] + P], m.xT[:, 0, 0:T],
                                    start=True, stop=True)
                ins.then_inc(dense_full, 1)

            def project_v(t):
                pe.wait_ge(dense_free, uses_before(t, "v"))
                for tt in range(TT):
                    ins = pe.matmul(dense[:, tt * D:(tt + 1) * D], m.xT[:, 0, tt * P:(tt + 1) * P],
                                    w[:, at["v"]:at["v"] + D], start=True, stop=True)
                ins.then_inc(dense_full, 1)

            def transpose_shift(b, t):
                pe.wait_ge(shift_split, b + 1)
                wait_apart(m, pe, dense_free, uses_before(t, "shift"))
                for qt in range(TT):
                    ins = pe.transpose(dense_b[0:PARTS * H, 0, qt * P:(qt + 1) * P],
                                       m.nm_parts[:, qt, :, :].rearrange("p s h -> p (s h)"), m.ident_b[:, :])
                ins.then_inc(dense_full, 1)

            def project_out(b, t):
                if soft:
                    pe.wait_ge(ocn_ready, b + 1)
                else:
                    pe.wait_ge(oc_loaded, (b + 1) * SEM)
                src = m.ocn if soft else m.oc
                pe.wait_ge(dense_free, uses_before(t, "proj"))
                for tt in range(TT):
                    ins = pe.matmul(dense[:, tt * D:(tt + 1) * D], src[:, tt * P:(tt + 1) * P],
                                    w[:, at["o"]:at["o"] + D], start=True, stop=True)
                ins.then_inc(dense_full, 1)

            def pass1(b, r, h):
                if h == 0:
                    pe.wait_ge(stack_loaded, (b + 1) * (7 * SEM))
                wait(pe, reduced, b * H + (h - 1))
                bank = score_banks[:, h % 2, :]
                for qt in range(TT):
                    q = m.qs[r][:, h, qt * P:(qt + 1) * P]
                    if soft:
                        ins = pe.matmul(bank[:, qt * T:(qt + 1) * T], q, m.ks[r][:, h, :], start=True, stop=True)
                    else:
                        first, n = qt * P, (qt + 1) * P
                        pe.matmul(bank[:, first:first + n], q, m.ks[r][:, h, 0:n], start=True, stop=True)
                        ins = pe.matmul(bank[:, first + n - P:first + n], m.ident_b[:, :], m.mask_b[:, :],
                                        start=False, stop=True, skip_group_check=True)
                ins.then_inc(scores_ready, 1)

            def pass2(b, r, p):
                if p == 0:
                    pe.wait_ge(shift_rows, (b + 1) * SEM)
                wait(pe, probs_ready, b * 8 + (p - 1))
                for n in range(2):
                    h = 2 * p + n
                    bank = shifted_banks[:, 2 * (p % 2) + n, :]
                    for kt in range(TT):
                        k = m.ks[r][:, h, kt * P:(kt + 1) * P]
                        if soft:
                            ins = pe.matmul(bank[:, kt * T:(kt + 1) * T], k, m.qs[r][:, h, :], start=True, stop=True)
                        else:
                            first = kt * T
                            pe.matmul(bank[:, first:first + T - kt * P], k, m.qs[r][:, h, kt * P:T],
                                      start=True, stop=True)
                            ins = pe.matmul(bank[:, first:first + P], m.ident_b[:, :], m.maskT_b[:, :],
                                            start=False, stop=True, skip_group_check=True)
                ins.then_inc(shifted_ready, 1)

            def pv(b, r, g):
                pe.wait_ge(probs_ready, b * 8 + (2 * g + 2))
                if g % 2 == 0:
                    wait(pe, ot_ready, b * 2 + g // 2)
                for kt in range(TT):
                    skip = 0 if soft else kt * P
                    for i in range(Q):
                        ins = pe.matmul(out_bank[32 * i:32 * i + 32, (g % 2) * T + skip:(g % 2 + 1) * T],
                                        m.v[r][:, kt, Q * g + i, :],
                                        m.pt[:, g % 2, i, kt * T:(kt + 1) * T - skip],
                                        start=(kt == 0), stop=(kt == TT - 1), skip_group_check=True)
                ins.then_inc(pv_done, 1)

            def slot(t, r):
                for h in range(H):
                    if live(t, 0):
                        if h == AT["xT"]:
                            transpose_x(t, t)
                        if h == AT["q"]:
                            project(t, "q", ["q", "qs"] if soft else ["q", "k"])
                        if soft and h == AT["k"]:
                            project(t, "k", ["k", "ks"])
                        if h == AT["v"]:
                            project_v(t)
                    if h == AT["shift"] and live(t, 2):
                        transpose_shift(t - 2, t)
                    if h == AT["proj"] and live(t, OUT):
                        project_out(t - OUT, t)
                    head, lag = head_of(h)
                    if live(t, lag):
                        pass1(t - lag, (r - lag) % RING, head)
                    if h % 2 == 1:
                        p, lag = pair_of(h // 2)
                        if live(t, lag):
                            pass2(t - lag, (r - lag) % RING, p)
                        if p % 2 == 0:
                            lag_pv, g = (lag, p // 2 - 1) if p else (lag + 1, 3)
                            if live(t, lag_pv):
                                pv(t - lag_pv, (r - lag_pv) % RING, g)

            def batch(b):
                transpose_x(b, b)
                project(b, "q", ["q", "k"])
                project_v(b)
                for h in range(H):
                    pass1(b, 0, h)
                transpose_shift(b, b)
                for p in range(H // 2):
                    pass2(b, 0, p)
                    if p % 2 == 1:
                        pv(b, 0, p // 2)
                project_out(b, b)

            if general:
                run_batches(pe, batch)
            else:
                run_slots(pe, slot)


def support_phase(nc, ctx, m):
    def sem(name):
        return ctx.enter_context(nc.semaphore(f"support_{name}"))

    flag_step = sem("flag_step")
    counted = sem("counted")

    with nc.Block() as block:
        @block.vector
        def _(dve):
            dve.tensor_reduce(m.flag[:, :], m.worst[:, :, :], AX.XY, ALU.max).then_inc(flag_step, 1)
            dve.wait_ge(flag_step, 1)
            dve.tensor_scalar(m.flag[:, :], m.flag[:, :], 0.0, None, ALU.is_gt).then_inc(flag_step, 1)
            dve.wait_ge(counted, 1)
            dve.tensor_scalar(m.redo[:, :], m.banks[0:1, 0, 0:1], 1.0, None, ALU.min).then_inc(flag_step, 1)
            dve.wait_ge(flag_step, 3)

        @block.tensor
        def _(pe):
            pe.wait_ge(flag_step, 2)
            pe.matmul(m.banks[0:1, 0, 0:1], m.flag[:, :], m.v[0][:, 0, 0, 8:9], start=True, stop=True)\
              .then_inc(counted, 1)


def feed_forward_phase(nc, ctx, m, name, x, out):
    N = 4
    SLOTS = B * TT // N
    NT = N * P

    def sem(what):
        return ctx.enter_context(nc.semaphore(f"{name}_{what}"))

    ln_stats = sem("ln_stats")
    var_ready = sem("var_ready")
    eps_added = sem("eps_added")
    rstd_ready = sem("rstd_ready")
    xhat_ready = sem("xhat_ready")
    turned = sem("turned")
    xT_ready = sem("xT_ready")
    gate_up = sem("gate_up")
    silu_ready = sem("silu_ready")
    hid_ready = sem("hid_ready")
    down_done = sem("down_done")
    x_done = sem("x_done")
    out_stored = sem("out_stored")

    ident = m.cc[:, CC["ident"]:CC["ident"] + P]
    turn_bank = m.banks[:, 0, :]
    gate_banks = m.banks[:, 1:3, :]
    up_banks = m.banks[:, 3:5, :]
    down_banks = m.banks[:, 5:7, :]
    gate_w, up_w, down_w = (m.wf[:, n * HIDDEN:(n + 1) * HIDDEN] for n in range(3))

    def live(t, lag):
        return not isinstance(t, int) or 0 <= t - lag < SLOTS

    def wait(eng, s, value):
        if not isinstance(value, int) or value > 0:
            eng.wait_ge(s, value)

    def run_slots(eng, slot):
        slot(0, 0)
        with eng.Fori(0, (SLOTS - 2) // 2) as n:
            slot(n * 2 + 1, 1)
            slot(n * 2 + 2, 0)
        slot(SLOTS - 1, (SLOTS - 1) % 2)
        slot(SLOTS, SLOTS % 2)

    with nc.Block() as block:

        @block.sync
        def _(sp):
            if out is not None:
                out_d = out.rearrange("b (t p) d -> p (b t) d", p=P)
                with sp.Fori(0, SLOTS) as t:
                    wait_apart(m, sp, x_done, t + 1)
                    sp.dma_start(out_d[:, bass.ds(t * N, N), :], x[:, bass.ds(t * N, N), :]).then_inc(out_stored, SEM)
                sp.wait_ge(out_stored, SLOTS * SEM)

        @block.gpsimd
        def _(pool):
            def rstd(t):
                wait_apart(m, pool, var_ready, t * N + N)
                pool.tensor_scalar(m.ve[:, 0:N], m.mv[:, 0:N, 1], EPS, None, ALU.add).then_inc(eps_added, 1)
                pool.wait_ge(eps_added, t + 1)
                wait(pool, xhat_ready, t * N)
                pool.tensor_tensor(m.rstd[:, 0:N], m.ve[:, 0:N], m.neghalf[:, 0:N], ALU.pow).then_inc(rstd_ready, 1)

            rstd(0)
            with pool.Fori(1, SLOTS) as t:
                rstd(t)

        @block.vector
        def _(dve):
            def layernorm_stats(t):
                wait(dve, xhat_ready, t * N)
                for n in range(N):
                    dve.bn_stats(m.stats[:, n, :], x[:, bass.ds(t * N + n, 1), :].rearrange("p o d -> p (o d)"))\
                       .then_inc(ln_stats, 1)
                wait_apart(m, dve, ln_stats, t * N + N)
                for n in range(N):
                    dve.bn_aggr(m.mv[:, n, :], m.stats[:, n, :]).then_inc(var_ready, 1)

            def layernorm_apply(t):
                dve.wait_ge(rstd_ready, t + 1)
                wait(dve, turned, t)
                for n in range(N):
                    dve.tensor_scalar(m.xhat[:, n, :], x[:, bass.ds(t * N + n, 1), :].rearrange("p o d -> p (o d)"),
                                      m.mv[:, n, 0:1], m.rstd[:, n:n + 1], ALU.subtract, ALU.mult)\
                       .then_inc(xhat_ready, 1)

            def hidden(t, r, c):
                dve.wait_ge(silu_ready, t * NC_H + (c + 1))
                k = (NC_H * r + c) % 2
                dve.tensor_tensor(m.hid[:, r, c, :], m.silu[:, k, :], up_banks[:, k, :], ALU.mult)\
                   .then_inc(hid_ready, 1)

            def residual(t, r):
                dve.wait_ge(down_done, t + 1)
                tiles = x[:, bass.ds(t * N, N), :]
                dve.tensor_tensor(tiles, down_banks[:, r, :].rearrange("p (n d) -> p n d", n=N), tiles, ALU.add)\
                   .then_inc(x_done, 1)

            def slot(t, r):
                if live(t, -1):
                    layernorm_stats(t + 1)
                if live(t, 0):
                    hidden(t, r, 0)
                if live(t, -1):
                    layernorm_apply(t + 1)
                if live(t, 0):
                    hidden(t, r, 1)
                if live(t, 1):
                    residual(t - 1, 1 - r)
                if live(t, 0):
                    hidden(t, r, 2)

            layernorm_stats(0)
            layernorm_apply(0)
            run_slots(dve, slot)

        @block.scalar
        def _(act):
            def take_xT(t, r):
                wait(act, gate_up, (t - 1) * NC_H)
                act.wait_ge(turned, t + 1)
                act.copy(m.xT[:, r, :], turn_bank).then_inc(xT_ready, 1)

            def silu(t, r, c):
                wait(act, hid_ready, t * NC_H + (c - 1))
                act.wait_ge(gate_up, t * NC_H + (c + 1))
                k = (NC_H * r + c) % 2
                act.activation(m.silu[:, k, :], gate_banks[:, k, :], ACT.Silu).then_inc(silu_ready, 1)

            def slot(t, r):
                if live(t, 0):
                    silu(t, r, 0)
                    silu(t, r, 1)
                if live(t, -1):
                    take_xT(t + 1, 1 - r)
                if live(t, 0):
                    silu(t, r, 2)

            take_xT(0, 0)
            run_slots(act, slot)

        @block.tensor
        def _(pe):
            def turn(t):
                pe.wait_ge(xhat_ready, t * N + N)
                wait(pe, xT_ready, t)
                for n in range(N):
                    ins = pe.transpose(turn_bank[:, n * P:(n + 1) * P], m.xhat[:, n, :], ident)
                ins.then_inc(turned, 1)

            def gate_and_up(t, r, c):
                if c == 0:
                    pe.wait_ge(xT_ready, t + 1)
                wait(pe, hid_ready, t * NC_H + (c - 1))
                k = (NC_H * r + c) % 2
                pe.matmul(gate_banks[:, k, :], gate_w[:, c * P:(c + 1) * P], m.xT[:, r, :], start=True, stop=True)
                pe.matmul(up_banks[:, k, :], up_w[:, c * P:(c + 1) * P], m.xT[:, r, :], start=True, stop=True)\
                  .then_inc(gate_up, 1)

            def down(t, r):
                pe.wait_ge(hid_ready, t * NC_H + NC_H)
                for n in range(N):
                    for c in range(NC_H):
                        ins = pe.matmul(down_banks[:, r, n * D:(n + 1) * D], m.hid[:, r, c, n * P:(n + 1) * P],
                                        down_w[:, c * D:(c + 1) * D], start=(c == 0), stop=(c == NC_H - 1))
                ins.then_inc(down_done, 1)

            def slot(t, r):
                if live(t, 0):
                    gate_and_up(t, r, 0)
                if live(t, 1):
                    down(t - 1, 1 - r)
                if live(t, 0):
                    gate_and_up(t, r, 1)
                if live(t, -1):
                    turn(t + 1)
                if live(t, 0):
                    gate_and_up(t, r, 2)

            turn(0)
            run_slots(pe, slot)


def stack_kernel(nc, io):
    with ExitStack() as ctx:
        m = allocate(nc, ctx)
        setup_phase(nc, ctx, m, io)
        attention_phase(nc, ctx, m, io, "a", m.x, m.x)
        feed_forward_phase(nc, ctx, m, "f1", m.x, None)
        attention_phase(nc, ctx, m, io, "b", m.x, m.x2)
        support_phase(nc, ctx, m)
        attention_phase(nc, ctx, m, io, "g", m.x, m.x2)
        feed_forward_phase(nc, ctx, m, "f2", m.x2, io["out"])


def shape_constants():
    f32 = np.float32
    c = np.zeros((P, CC_COLS), f32)
    c[:, CC["ident"]:CC["ident"] + P] = np.eye(P, dtype=f32)
    inv = f32(1.0) / f32(10000.0) ** (np.arange(0, HD, 2, dtype=f32) / f32(HD))
    freqs = np.arange(T, dtype=f32)[:, None] * inv[None, :]
    emb = np.concatenate([freqs, freqs], axis=-1)
    cos, sin = np.cos(emb).astype(f32).T, np.sin(emb).astype(f32).T
    sign = np.where(np.arange(HD) % 2 == 0, f32(-1.0), f32(1.0))[:, None]
    c[:, CC["cos"]:CC["cos"] + T] = np.repeat(cos, H, axis=0)
    c[:, CC["sin"]:CC["sin"] + T] = np.repeat(sin * sign, H, axis=0)
    q, k = np.arange(P)[:, None], np.arange(P)[None, :]
    c[:, CC["mask"]:CC["mask"] + P] = np.where(k > q, f32(NEG), f32(0.0))
    c[:, CC["maskT"]:CC["maskT"] + P] = np.where(q > k, f32(NEG), f32(0.0))
    c[:, CC["invk"]:CC["invk"] + 256] = np.tile(f32(1.0) / np.arange(1, 9, dtype=f32), 32)
    c[:, CC["seg"]:CC["seg"] + 256] = np.tile(np.arange(8) > 0, 32)
    return c


def kernel(**inputs):
    import concourse.bacc as _bacc
    from concourse.bass_utils import run_bass_kernel_spmd as _run

    a = {n: np.asarray(v) for n, v in inputs.items()}
    dm = np.arange(D).reshape(H, HD).T.reshape(-1)
    dms = np.arange(D).reshape(H, HD)[:, np.arange(HD) ^ 1].T.reshape(-1)
    idg = np.arange(D).reshape(Q, Q, HD).transpose(1, 2, 0).reshape(-1)

    def spread(v):
        return np.broadcast_to(v, (P, D))

    wa = np.concatenate([
        a["L0_attn_a_Wq"].T[:, dm], a["L0_attn_a_Wq"].T[:, dms], a["L0_attn_a_Wk"].T[:, dm],
        a["L0_attn_a_Wk"].T[:, dms], a["L0_attn_a_Wv"].T, a["L0_attn_a_Wo"].T[idg],
        a["L0_attn_a_bq"][dm, None], a["L0_attn_a_bq"][dms, None], a["L0_attn_a_bk"][dm, None],
        a["L0_attn_a_bk"][dms, None], spread(a["L0_attn_a_bv"]), spread(a["L0_attn_a_bo"])], axis=1)
    wat, bat = a["L0_attn_b_w_attn"], a["L0_attn_b_b_attn"]
    wb = np.concatenate([
        wat[:, 0:D][:, dm], wat[:, D:2 * D][:, dm], wat[:, 2 * D:], a["L0_attn_b_w_proj"][idg],
        bat[0:D][dm, None], bat[D:2 * D][dm, None], spread(bat[2 * D:]), spread(a["L0_attn_b_b_proj"])], axis=1)
    wf = np.concatenate([
        a["L0_ffn_w_gate"].T, a["L0_ffn_w_up"].T,
        a["L0_ffn_w_down"].T.reshape(NC_H, P, D).transpose(1, 0, 2).reshape(P, HIDDEN)], axis=1)
    arrays = {"x": a["L0_attn_a_x"], "wa": wa, "wb": wb, "wf": wf, "consts": shape_constants()}
    arrays = {n: np.ascontiguousarray(v) for n, v in arrays.items()}

    nc = _bacc.Bacc("TRN2", target_bir_lowering=False, num_devices=1)
    io = {n: nc.dram_tensor(n + "_in", v.shape, mybir.dt.from_np(v.dtype), kind="ExternalInput").ap()
          for n, v in arrays.items()}
    io["out"] = nc.dram_tensor("out_0", (B, T, D), F32, kind="ExternalOutput").ap()
    stack_kernel(nc, io)
    r = _run(nc, [{n + "_in": v for n, v in arrays.items()}], core_ids=[0])
    return r.results[0]["out_0"]
```
